# Optimizing a Trainium2 kernel written in Bass

```python
import numpy as np
import jax
import jax.numpy as jnp

def _softmax(x, axis=-1):
    return jax.nn.softmax(x, axis=axis)

def _gelu(x):
    return jax.nn.gelu(x, approximate=True)

def _silu(x):
    return jax.nn.silu(x)

def _sigmoid(x):
    return jax.nn.sigmoid(x)

def _layernorm(x, axis=-1, eps=1e-05):
    m = jnp.mean(x, axis=axis, keepdims=True)
    v = jnp.var(x, axis=axis, keepdims=True)
    return (x - m) / jnp.sqrt(v + eps)

def _scatter_add(tgt, idx, src, axis=0):
    return tgt.at[idx].add(src)

def _segment_sum(src, seg, n):
    return jax.ops.segment_sum(src, seg, n)
kernel_name = 'mk_adj_preln_d2_adj_r2_f0a128'

def setup_inputs(seed: int=0):
    np.random.seed(seed)
    _w = jnp.asarray

    def _rec_inputs():
        import jax
        import jax.numpy as jnp
        _gk = jax.random.key(seed)
        x = -0.0005207 + 1.001 * jax.random.normal(jax.random.fold_in(_gk, 1), (3327, 256), jnp.float32)
        _a = jax.random.bernoulli(jax.random.fold_in(_gk, 2), 0.00961827, (3327, 3327))
        _a = jnp.logical_or(_a, jnp.eye(3327, dtype=bool))
        _af = _a.astype(jnp.float32)
        _af = _af * jax.random.uniform(jax.random.fold_in(_gk, 3), (3327, 3327), jnp.float32, 0.05, 1)
        adj = _af
        return (x, adj)
    x, adj = _rec_inputs()

    def _L0_gnn_setup():
        import jax, jax.numpy as jnp
        import numpy as np
        N, D_IN, D_ATTN, STEPS, P_NUC, TAU = (2048, 256, 64, 2, 0.9, 1.0)
        LN_EPS = 1e-05

        def _xavier(key, shape):
            fan_in, fan_out = (shape[-2], shape[-1])
            lim = np.sqrt(6.0 / (fan_in + fan_out))
            return jax.random.uniform(key, shape, jnp.float32, -lim, lim)

        def _adj_from_feats(Xa, W1, W2, W3):
            Q = Xa @ W1
            K = Xa @ W3
            logits = Q @ W2 @ K.T / TAU
            idx = jnp.argsort(-logits, axis=1)
            vals = jnp.take_along_axis(logits, idx, axis=1)
            csum = jnp.cumsum(jax.nn.softmax(vals, axis=1), axis=1)
            k_i = jnp.sum(csum < P_NUC, axis=1) + 1
            ranks = jnp.arange(logits.shape[1])[None, :]
            keep_sorted = ranks < k_i[:, None]
            inv = jnp.argsort(idx, axis=1)
            keep = jnp.take_along_axis(keep_sorted, inv, axis=1)
            masked = jnp.where(keep, logits, -jnp.inf)
            return jax.nn.softmax(masked, axis=1)
        key = jax.random.key(seed)
        ks = jax.random.split(key, 9)
        return {'X': jax.random.normal(ks[0], (N, D_IN), jnp.float32), 'S': jax.random.uniform(ks[1], (N, N), jnp.float32), 'W1': _xavier(ks[2], (D_IN, D_ATTN)), 'W2': _xavier(ks[3], (D_ATTN, D_ATTN)), 'W3': _xavier(ks[4], (D_IN, D_ATTN)), 'U1': _xavier(ks[5], (STEPS, D_IN, D_IN)), 'U2': _xavier(ks[6], (STEPS, D_IN, D_IN)), 'U3': _xavier(ks[7], (STEPS, D_IN, D_IN)), 'gamma': jnp.ones((D_IN,), jnp.float32), 'beta': jnp.zeros((D_IN,), jnp.float32)}
    _L0_gnn_all = _L0_gnn_setup()
    _L0_gnn_in = {k: v for k, v in _L0_gnn_all.items() if k in ('W1', 'W2', 'W3', 'U1', 'U2', 'U3', 'gamma', 'beta')}
    del _L0_gnn_all

    def _L1_gnn_setup():
        import jax, jax.numpy as jnp
        import numpy as np
        N = 3072
        D_IN = 256
        D_OUT = 256
        DENSITY = 0.005
        key = jax.random.key(seed)
        ks = jax.random.split(key, 12)
        x = jax.random.normal(ks[0], (N, D_IN), dtype=jnp.float32)
        adj_a = (jax.random.uniform(ks[1], (N, N)) < DENSITY).astype(jnp.float32)
        adj_b = (jax.random.uniform(ks[2], (N, N)) < DENSITY).astype(jnp.float32)
        W_sa = jax.random.normal(ks[3], (D_IN, D_OUT), dtype=jnp.float32) * (1.414 / np.sqrt(D_IN + D_OUT))
        a_sa = jax.random.normal(ks[4], (1, 2 * D_OUT), dtype=jnp.float32) * (1.414 / np.sqrt(1 + 2 * D_OUT))
        stdv = 1.0 / np.sqrt(D_OUT)
        W_gcnb = jax.random.uniform(ks[5], (D_IN, D_OUT), minval=-stdv, maxval=stdv, dtype=jnp.float32)
        b_gcnb = jax.random.uniform(ks[6], (D_OUT,), minval=-stdv, maxval=stdv, dtype=jnp.float32)
        s = 1.0 / np.sqrt(2 * D_IN)
        Wa = jax.random.uniform(ks[7], (1, 2 * D_IN), minval=-s, maxval=s, dtype=jnp.float32)
        ba = jax.random.uniform(ks[8], (1,), minval=-s, maxval=s, dtype=jnp.float32)
        Wb = jax.random.uniform(ks[9], (1, 2 * D_IN), minval=-s, maxval=s, dtype=jnp.float32)
        bb = jax.random.uniform(ks[10], (1,), minval=-s, maxval=s, dtype=jnp.float32)
        return {'x': x, 'adj_a': adj_a, 'adj_b': adj_b, 'W_sa': W_sa, 'a_sa': a_sa, 'W_gcnb': W_gcnb, 'b_gcnb': b_gcnb, 'Wa': Wa, 'ba': ba, 'Wb': Wb, 'bb': bb}
    _L1_gnn_all = _L1_gnn_setup()
    _L1_gnn_in = {k: v for k, v in _L1_gnn_all.items() if k in ('W_sa', 'a_sa', 'W_gcnb', 'b_gcnb', 'Wa', 'ba', 'Wb', 'bb')}
    del _L1_gnn_all
    return {'x': x, 'adj': adj, 'L0_gnn_W1': _L0_gnn_in['W1'], 'L0_gnn_W2': _L0_gnn_in['W2'], 'L0_gnn_W3': _L0_gnn_in['W3'], 'L0_gnn_U1': _L0_gnn_in['U1'], 'L0_gnn_U2': _L0_gnn_in['U2'], 'L0_gnn_U3': _L0_gnn_in['U3'], 'L0_gnn_gamma': _L0_gnn_in['gamma'], 'L0_gnn_beta': _L0_gnn_in['beta'], 'L1_gnn_W_sa': _L1_gnn_in['W_sa'], 'L1_gnn_a_sa': _L1_gnn_in['a_sa'], 'L1_gnn_W_gcnb': _L1_gnn_in['W_gcnb'], 'L1_gnn_b_gcnb': _L1_gnn_in['b_gcnb'], 'L1_gnn_Wa': _L1_gnn_in['Wa'], 'L1_gnn_ba': _L1_gnn_in['ba'], 'L1_gnn_Wb': _L1_gnn_in['Wb'], 'L1_gnn_bb': _L1_gnn_in['bb']}

def reference(x, adj, L0_gnn_W1, L0_gnn_W2, L0_gnn_W3, L0_gnn_U1, L0_gnn_U2, L0_gnn_U3, L0_gnn_gamma, L0_gnn_beta, L1_gnn_W_sa, L1_gnn_a_sa, L1_gnn_W_gcnb, L1_gnn_b_gcnb, L1_gnn_Wa, L1_gnn_ba, L1_gnn_Wb, L1_gnn_bb):
    import jax
    import jax.numpy as jnp

    def _L0_gnn_ref(X, S, W1, W2, W3, U1, U2, U3, gamma, beta):
        import jax, jax.numpy as jnp
        import numpy as np
        N, D_IN, D_ATTN, STEPS, P_NUC, TAU = (2048, 256, 64, 2, 0.9, 1.0)
        LN_EPS = 1e-05

        def _xavier(key, shape):
            fan_in, fan_out = (shape[-2], shape[-1])
            lim = np.sqrt(6.0 / (fan_in + fan_out))
            return jax.random.uniform(key, shape, jnp.float32, -lim, lim)

        def _adj_from_feats(Xa, W1, W2, W3):
            Q = Xa @ W1
            K = Xa @ W3
            logits = Q @ W2 @ K.T / TAU
            idx = jnp.argsort(-logits, axis=1)
            vals = jnp.take_along_axis(logits, idx, axis=1)
            csum = jnp.cumsum(jax.nn.softmax(vals, axis=1), axis=1)
            k_i = jnp.sum(csum < P_NUC, axis=1) + 1
            ranks = jnp.arange(logits.shape[1])[None, :]
            keep_sorted = ranks < k_i[:, None]
            inv = jnp.argsort(idx, axis=1)
            keep = jnp.take_along_axis(keep_sorted, inv, axis=1)
            masked = jnp.where(keep, logits, -jnp.inf)
            return jax.nn.softmax(masked, axis=1)
        n = X.shape[0]
        S = S + jnp.eye(n, dtype=X.dtype)
        Rf = S / jnp.clip(S.sum(axis=1, keepdims=True), 1e-12)
        Rb = S / jnp.clip(S.sum(axis=0), 1e-12)[:, None]
        Xf, Xb, Xa = (X, X, X)
        Z = jnp.zeros_like(X)
        for s in range(STEPS):
            A = _adj_from_feats(Xa, W1, W2, W3)
            Xf = Rf @ Xf
            Xb = Rb @ Xb
            Xa = A @ Xa
            Z = Z + (Xf @ U1[s] + Xb @ U2[s] + Xa @ U3[s])
        Y = X + Z
        mu = Y.mean(axis=-1, keepdims=True)
        var = Y.var(axis=-1, keepdims=True)
        return (Y - mu) / jnp.sqrt(var + LN_EPS) * gamma + beta

    def _L1_gnn_ref(x, adj_a, adj_b, W_sa, a_sa, W_gcnb, b_gcnb, Wa, ba, Wb, bb):
        import jax, jax.numpy as jnp
        import numpy as np
        N = 3072
        D_IN = 256
        D_OUT = 256
        DENSITY = 0.005
        type_sum_a = adj_a @ x
        type_sum_b = adj_b @ x
        attn_a = jax.nn.sigmoid(jnp.concatenate([type_sum_a, x], axis=1) @ Wa.T + ba)
        attn_b = jax.nn.sigmoid(jnp.concatenate([type_sum_b, x], axis=1) @ Wb.T + bb)
        h = x @ W_sa
        Hd = h.shape[1]
        s_left = h @ a_sa[0, :Hd]
        s_right = h @ a_sa[0, Hd:]
        scores = s_left[:, None] + s_right[None, :]
        e = jnp.where(adj_a != 0, jnp.exp(-jax.nn.leaky_relu(scores, 0.01)), 0.0)
        attn = e / (jnp.sum(e, axis=1, keepdims=True) + 1e-05)
        x_a = attn @ h
        x_b = adj_b @ (x @ W_gcnb) + b_gcnb
        return jax.nn.sigmoid(attn_a * x_a + attn_b * x_b)
    h = jnp.maximum(_layernorm(x, axis=-1), 0.0)
    x = x + _L0_gnn_ref(h, adj, L0_gnn_W1, L0_gnn_W2, L0_gnn_W3, L0_gnn_U1, L0_gnn_U2, L0_gnn_U3, L0_gnn_gamma, L0_gnn_beta)
    h = jnp.maximum(_layernorm(x, axis=-1), 0.0)
    x = x + _L1_gnn_ref(h, adj, adj, L1_gnn_W_sa, L1_gnn_a_sa, L1_gnn_W_gcnb, L1_gnn_b_gcnb, L1_gnn_Wa, L1_gnn_ba, L1_gnn_Wb, L1_gnn_bb)
    return x

_drawn_inputs = setup_inputs


def setup_inputs(seed=0):
    import zlib

    import numpy as np

    out = dict(_drawn_inputs(seed))
    spreads = {'L0_gnn_gamma': (1.0, 0.2), 'L0_gnn_beta': (0.0, 0.1)}
    factors = {'L1_gnn_W_sa': 23.228, 'L1_gnn_a_sa': 54.537, 'L1_gnn_b_gcnb': 40.064, 'L1_gnn_Wa': 29.264}
    for name, (base, spread) in spreads.items():
        noise = np.random.default_rng([zlib.crc32(name.encode()), seed]).standard_normal(out[name].shape)
        drawn = base * np.exp(spread * noise) if base else spread * noise
        out[name] = jnp.asarray(drawn.astype(out[name].dtype))
    for name, factor in factors.items():
        out[name] = (out[name] * factor).astype(out[name].dtype)
    return out
```

```python
from contextlib import ExitStack

import numpy as np
import concourse.bass as bass
from concourse import mybir

F32 = mybir.dt.float32
U8 = mybir.dt.uint8
I32 = mybir.dt.int32
ALU = mybir.AluOpType
ACT = mybir.ActivationFunctionType
AX = mybir.AxisListType.X

P = 128
N = 3327
NT = -(-N // P)
NP = NT * P
D = 256
DA = 64
W = D + 2
HALF = NT // 2
LC = 512
NL = -(-N // LC)
AC = -(-NT // 4)
PAIRS = NT // 2
P_NUC = 0.9
LN_EPS = 1e-5
CLIP = 1e-12
SIG_MIN = -87.0

FLOOR = (1.0 - P_NUC) * 0.999 / N
SPAN = 1.01 / FLOOR
FAST_STEPS = (8, 12)
EXACT_STEPS = 24
EXACT_ROUNDS = 4
SLACK = 4e-6


def chunk_base(step):
    return (NT, NT + 8 * NT, NT + 18 * NT)[step]


def build(nc, x, adj_t, adj_n, w1t, w2, w3, u_all, wh, wg, rows, gate_bias, out):
    V = nc.vector
    with ExitStack() as ctx:
        def sb(name, shape, dt=F32):
            return ctx.enter_context(nc.sbuf_tensor(name, shape, dt))

        def ps(name, shape):
            return ctx.enter_context(nc.psum_tensor(name, shape, F32))

        def sem(name):
            return ctx.enter_context(nc.semaphore(name))

        xs = sb("xs", [P, NT * W])
        fb = sb("fb", [P, NT * 2 * D])
        xa = sb("xa", [P, NT * W])
        kq = [sb(f"kq{s}", [P, NP]) for s in range(2)]
        e_buf = [sb(f"e{i}", [P, NP]) for i in range(2)]
        a_buf = sb("a_buf", [P, NP])
        ring = sb("ring", [P, 2, HALF * P])
        tr = [sb(f"tr{i}", [P, 4 * P]) for i in range(2)]
        junk = sb("junk", [P, NP], U8)
        stage = sb("stage", [P, 6 * D])
        ident = sb("ident", [P, P])
        ones = sb("ones", [P, P])
        diag = sb("diag", [P, P])
        wqk = sb("wqk", [P, 2 * P])
        w1t_sb = sb("w1t_sb", [DA, D])
        w2_sb = sb("w2_sb", [DA, DA])
        q_st = [sb(f"q_st{i}", [DA, P]) for i in range(2)]
        neg_max = [sb(f"neg_max{i}", [P, 1]) for i in range(2)]
        z = [sb(f"z{i}", [P, 1]) for i in range(2)]
        inv_kept = [sb(f"inv_kept{i}", [P, 1]) for i in range(2)]
        inv_sum = sb("inv_sum", [P, 2])
        inv_sums = sb("inv_sums", [P, 2 * NT])
        tgt = sb("tgt", [P, 2])
        lo = sb("lo", [P, 1])
        hi = sb("hi", [P, 1])
        mid = sb("mid", [P, 1])
        wid = sb("wid", [P, 1])
        inc = sb("inc", [P, 1])
        mass = sb("mass", [P, 1])
        above = sb("above", [P, 1])
        top8 = sb("top8", [P, 8])
        cum8 = sb("cum8", [P, 8])
        tau = sb("tau", [P, 1])
        kept = sb("kept", [P, 1])
        bad = sb("bad", [P, 2])
        flag = sb("flag", [P, 32])
        flag_t = sb("flag_t", [P, 32])
        flag_i = sb("flag_i", [P, 1], I32)
        bst = sb("bst", [P, 6])
        mv = sb("mv", [P, 2])
        mvs = sb("mvs", [P, 2 * NT])
        std = sb("std", [P, NT])
        rstd = sb("rstd", [P, NT])
        shift = sb("shift", [P, NT])
        n_sr = sb("n_sr", [P, NT])
        n_s = sb("n_s", [P, 2])
        hb = sb("hb", [P, 2 * NT])
        gate = sb("gate", [P, 4])
        den = sb("den", [P, 1])
        gb_sb = sb("gb_sb", [P, 2])
        x1 = fb[:, 0:NT * D]
        slb = fb[:, NT * D:NT * D + NP]
        hh = xa
        u_sb = kq[0][:, 0:6 * 2 * D]
        flat_ring = ring[:, :, :].rearrange("p a b -> p (a b)")
        wh_sb = flat_ring[:, 0:2 * W]
        wg_sb = flat_ring[:, 2 * W:4 * W]
        rows_sb = flat_ring[:, 4 * W:4 * W + 5 * D]
        gamma, beta, a_left, a_right, b_gcn = (rows_sb[:, i * D:(i + 1) * D] for i in range(5))
        ts_st = stage[:, 0:D]
        h_st = stage[:, D:2 * D]
        work = stage[:, 2 * D:3 * D]
        work2 = stage[:, 3 * D:4 * D]
        out_st = [stage[:, 4 * D:5 * D], stage[:, 5 * D:6 * D]]

        bank_l = [ps(f"bank_l{i}", [P, LC]) for i in range(3)]
        bank_t = [ps(f"bank_t{i}", [P, LC]) for i in range(2)]
        bank_xa = ps("bank_xa", [P, LC])
        bank_s = ps("bank_s", [P, LC])
        bank_m = ps("bank_m", [P, LC])

        x_in = sem("x_in")
        w_in = sem("w_in")
        wqk_in = sem("wqk_in")
        u_in = sem("u_in")
        late_in = sem("late_in")
        const_ready = sem("const_ready")
        stats_ready = sem("stats_ready")
        std_ready = sem("std_ready")
        rstd_ready = sem("rstd_ready")
        h_ready = sem("h_ready")
        w12_done = sem("w12_done")
        w12_ready = sem("w12_ready")
        tr_done = sem("tr_done")
        tr_ready = sem("tr_ready")
        tr_used = sem("tr_used")
        kq_ready = sem("kq_ready")
        q_in = [sem(f"q_in{i}") for i in range(2)]
        l_done = sem("l_done")
        l_copied = sem("l_copied")
        max_ready = sem("max_ready")
        exp_ready = sem("exp_ready")
        a_ready = sem("a_ready")
        xa_ready = sem("xa_ready")
        adj_in = [sem(f"adj_in{i}") for i in range(2)]
        adj_used = sem("adj_used")
        inv_ready = sem("inv_ready")
        s_ready = sem("s_ready")
        y_ready = sem("y_ready")
        hh_read = sem("hh_read")
        diag_ready = sem("diag_ready")
        sl_done = sem("sl_done")
        sl_ready = sem("sl_ready")
        hh_ready = sem("hh_ready")
        full_in = [sem(f"full_in{i}") for i in range(2)]
        score_ready = sem("score_ready")
        score_exp = sem("score_exp")
        et_ready = sem("et_ready")
        ts_done = sem("ts_done")
        ts_ready = sem("ts_ready")
        att_done = sem("att_done")
        gate_arg = sem("gate_arg")
        gate_exp = sem("gate_exp")
        comb_ready = sem("comb_ready")
        comb_exp = sem("comb_exp")
        out_ready = sem("out_ready")
        out_sent = [sem(f"out_sent{i}") for i in range(2)]

        block = ctx.enter_context(nc.Block())

        def steps(eng, iteration):
            iteration(0, 0, True, False)
            with eng.Fori(0, PAIRS - 1) as pr:
                iteration(2 * pr + 1, 1, True, True)
                iteration(2 * pr + 2, 0, True, True)
            iteration(NT - 1, 1, True, True)
            iteration(NT, 0, False, True)

        @block.sync
        def _(sp):
            for u in range(2):
                sp.sem_inc(out_sent[u], 16)
            for from_one in (kq_ready, xa_ready, a_ready, y_ready, hh_ready, hh_read, sl_done, sl_ready, ts_ready):
                sp.sem_inc(from_one, 1)
            sp.dma_start(x1, x).then_inc(x_in, 16)
            sp.dma_start(w1t_sb[:, :], w1t).then_inc(w_in, 16)
            sp.dma_start(w2_sb[:, :], w2).then_inc(w_in, 16)
            for c in range(2):
                sp.dma_start(wqk[:, c * P:c * P + DA], w3[c * P:(c + 1) * P, :]).then_inc(wqk_in, 16)

            def load_q(step, k, par):
                sp.dma_start(q_st[par][:, :], kq[step][DA:P, bass.ds(k * P, P)]).then_inc(q_in[par], 16)

            def load_adj(src, k, half, piece):
                sp.wait_ge(adj_used, piece + 1)
                sp.dma_start(ring[:, half, :], src[bass.ds(2 * k + half, 1), :, :].rearrange(
                    "a p n -> (a p) n")).then_inc(adj_in[half], 16)

            def pieces(step, k):
                if step == 0:
                    for j, src in enumerate((adj_t, adj_t, adj_n, adj_n)):
                        load_adj(src, k, j % 2, 4 * k + j)
                else:
                    for half in range(2):
                        load_adj(adj_t, k, half, 4 * NT + 2 * k + half)

            for step in range(2):
                sp.wait_ge(kq_ready, 1 + (step + 1) * NT)
                load_q(step, 0, 0)
                load_q(step, 1, 1)
                if step == 1:
                    sp.wait_ge(l_done, NL * NT)
                    sp.dma_start(u_sb, u_all).then_inc(u_in, 16)
                with sp.Fori(0, PAIRS - 1) as pr:
                    for u in range(2):
                        pieces(step, 2 * pr + u)
                        sp.wait_ge(l_done, NL * (step * NT + 2 * pr + u + 1))
                        load_q(step, 2 * pr + u + 2, u)
                for u in range(2):
                    pieces(step, NT - 2 + u)
            sp.wait_ge(adj_used, 6 * NT + 2)
            sp.wait_ge(y_ready, 1 + NT)
            sp.dma_start(wh_sb, wh).then_inc(late_in, 16)
            sp.dma_start(wg_sb, wg).then_inc(late_in, 16)
            sp.dma_start(rows_sb, rows).then_inc(late_in, 16)
            sp.dma_start(gb_sb[:, :], gate_bias).then_inc(late_in, 16)
            sp.dma_start(x1, x).then_inc(x_in, 16)

            def load_full(k, par):
                for half in range(2):
                    sp.dma_start(e_buf[par][:, half * HALF * P:(half + 1) * HALF * P],
                                 adj_t[bass.ds(2 * k + half, 1), :, :].rearrange("a p n -> (a p) n")
                                 ).then_inc(full_in[par], 16)

            def store(k, par):
                sp.wait_ge(out_ready, k + 1)
                sp.dma_start(out[bass.ds(k * P, P), :], out_st[par]).then_inc(out_sent[par], 16)

            sp.wait_ge(a_ready, 1 + 2 * NT)
            sp.wait_ge(tr_ready, chunk_base(2) + 2)
            load_full(0, 0)
            load_full(1, 1)
            with sp.Fori(0, PAIRS - 1) as pr:
                for u in range(2):
                    sp.wait_ge(et_ready, 2 * pr + u + 1)
                    sp.wait_ge(ts_done, 2 * pr + u + 1)
                    load_full(2 * pr + u + 2, u)
                    store(2 * pr + u, u)
            store(NT - 2, 0)
            sp.wait_ge(out_ready, NT)
            sp.dma_start(out[(NT - 1) * P:N, :], out_st[1][0:N - (NT - 1) * P, :]).then_inc(out_sent[1], 16)
            for u in range(2):
                sp.wait_ge(out_sent[u], 16 + 16 * PAIRS)

        @block.gpsimd
        def _(pool):
            nc.gpsimd.memset(ident[:, :], 0.0)
            nc.gpsimd.memset(ones[:, :], 1.0)
            nc.gpsimd.memset(flag[:, :], 0.0)
            for e in e_buf:
                nc.gpsimd.memset(e[:, N:NP], 0.0)
            for rows_with_ones in (xs, xa):
                cols = rows_with_ones[:, :].rearrange("p (k w) -> p k w", w=W)
                nc.gpsimd.memset(cols[:, :, D:W], 1.0)
            pool.drain()
            nc.gpsimd.affine_select(out=ident[:, :], in_=ident[:, :], compare_op=ALU.not_equal, fill=1.0,
                                    base=0, pattern=[[-1, P]], channel_multiplier=1)
            pool.drain().then_inc(const_ready, 1)

        @block.tensor
        def _(pe):
            mm = nc.tensor.matmul
            pe.sem_inc(adj_used, 2)
            pe.sem_inc(tr_used, 2)
            pe.sem_inc(att_done, 2)
            pe.wait_ge(const_ready, 1)
            pe.wait_ge(w_in, 32)
            for c in range(2):
                last = mm(bank_m[:, c * DA:(c + 1) * DA], w1t_sb[:, c * P:(c + 1) * P], w2_sb[:, :],
                          start=True, stop=True)
            last.then_inc(w12_done, 1)
            pe.wait_ge(w12_ready, 1)
            pe.wait_ge(wqk_in, 32)

            def transpose_chunk(g, par, blocks):
                pe.wait_ge(tr_ready, g + 1)
                for b, source in enumerate(blocks):
                    last = nc.tensor.transpose(bank_t[par][:, b * P:(b + 1) * P], source, ident[:, :])
                last.then_inc(tr_done, 1)

            def use_chunk(g, par, products):
                pe.wait_ge(tr_ready, g + 3)
                for o, b, other, start, stop in products:
                    last = mm(o, tr[par][:, b * P:(b + 1) * P], other, start=start, stop=stop)
                last.then_inc(tr_used, 1)

            def two_blocks(rows):
                return rows[:, 0:P], rows[:, P:2 * P]

            def project_kq(g, par, m):
                pe.wait_ge(tr_ready, g + 3)
                pe.wait_ge(kq_ready, 1 + m)
                for c in range(2):
                    last = mm(bank_m[:, 0:P], wqk[:, c * P:(c + 1) * P], tr[par][:, c * P:(c + 1) * P],
                              start=(c == 0), stop=(c == 1))
                last.then_inc(tr_used, 1)

            with pe.Fori(0, PAIRS) as pr:
                for u in range(2):
                    pe.wait_ge(h_ready, 2 * pr + u + 1)
                    transpose_chunk(2 * pr + u, u, two_blocks(stage[:, 5 * D:6 * D]))
                    project_kq(2 * pr + u, u, 2 * pr + u)

            def logits(step, k, par):
                n = step * NT + k
                pe.wait_ge(q_in[par], 16 * (step * PAIRS + k // 2 + 1))
                for c in range(NL):
                    width = min(LC, N - c * LC)
                    pe.wait_ge(l_copied, NL * n + c - 2 if c >= 3 else NL * n)
                    mm(bank_l[c % 3][:, 0:width], q_st[par][:, :], kq[step][0:DA, c * LC:c * LC + width],
                       start=True, stop=True).then_inc(l_done, 1)

            def s_product(step, k):
                pe.wait_ge(s_ready, step * NT + k)
                src, row, width = (xs, W, D + 1) if step == 0 else (fb, 2 * D, 2 * D)
                mm(bank_s[:, 0:width], ident[:, :], src[:, bass.ds(k * row, width)], start=True, stop=False)
                for half in range(2):
                    pe.wait_ge(adj_in[half], 16 * (2 * k + 1 if step == 0 else 2 * NT + k + 1))
                    for b in range(HALF):
                        j = half * HALF + b
                        last = mm(bank_s[:, 0:width], ring[:, half, b * P:(b + 1) * P],
                                  src[:, j * row:j * row + width], start=False, stop=(j == NT - 1))
                    last.then_inc(adj_used, 1)
                if step == 0:
                    mm(bank_s[:, D + 2:D + 3], ident[:, :], ones[:, 0:1], start=True, stop=False)
                    for half in range(2):
                        pe.wait_ge(adj_in[half], 16 * (2 * k + 2))
                        for b in range(HALF):
                            last = mm(bank_s[:, D + 2:D + 3], ring[:, half, b * P:(b + 1) * P], ones[:, 0:1],
                                      start=False, stop=(half == 1 and b == HALF - 1))
                        last.then_inc(adj_used, 1)

            def a_product(step, k):
                n = step * NT + k
                g = chunk_base(step) + (8 if step == 0 else 10) * k
                src = xs if step == 0 else xa
                pe.wait_ge(a_ready, 1 + n + 1)

                def product(c):
                    if c == 0:
                        pe.wait_ge(xa_ready, 1 + n)
                    use_chunk(g + c, c % 2, [(bank_xa[:, 0:D], j % 4, src[:, j * W:j * W + D],
                                              j == 0, j == NT - 1) for j in range(4 * c, min(4 * c + 4, NT))])

                for c in range(AC):
                    transpose_chunk(g + c, c % 2, [a_buf[:, j * P:(j + 1) * P]
                                                   for j in range(4 * c, min(4 * c + 4, NT))])
                    if c:
                        product(c - 1)
                product(AC - 1)
                if step == 0:
                    pe.wait_ge(xa_ready, 1 + n + 1)
                    transpose_chunk(g + 7, 1, two_blocks(stage[:, 5 * D:6 * D]))
                    project_kq(g + 7, 1, NT + k)
                    return

                def four_blocks(c):
                    return [stage[:, (4 * c + b) * P:(4 * c + b + 1) * P] for b in range(4)]

                def z_product(c):
                    use_chunk(g + 7 + c, (7 + c) % 2,
                              [(bank_m[:, 0:D], b, u_sb[:, (4 * c + b) * D:(4 * c + b + 1) * D],
                                c == 0 and b == 0, c == 2 and b == 3) for b in range(4)])

                pe.wait_ge(s_ready, n + 1)
                pe.wait_ge(u_in, 16)
                pe.wait_ge(kq_ready, 1 + 2 * NT)
                pe.wait_ge(y_ready, 1 + k)
                transpose_chunk(g + 7, 1, four_blocks(0))
                transpose_chunk(g + 8, 0, four_blocks(1))
                z_product(0)
                pe.wait_ge(xa_ready, 1 + n + 1)
                transpose_chunk(g + 9, 1, four_blocks(2))
                z_product(1)
                z_product(2)

            for step in range(2):
                def iteration(k, par, begins, ends):
                    if begins:
                        logits(step, k, par)
                        s_product(step, k)
                    if ends:
                        a_product(step, k - 1)

                steps(pe, iteration)

            pe.wait_ge(late_in, 64)
            with pe.Fori(0, PAIRS) as pr:
                for u in range(2):
                    k = 2 * pr + u
                    g = chunk_base(2) + k
                    pe.wait_ge(h_ready, NT + k + 1)
                    transpose_chunk(g, u, two_blocks(h_st))
                    pe.wait_ge(hh_ready, 1 + k)
                    pe.wait_ge(hh_read, 1 + k)
                    use_chunk(g, u, [(bank_s[:, 0:W], c, wh_sb[:, c * W:(c + 1) * W], c == 0, c == 1)
                                     for c in range(2)])
                    pe.wait_ge(diag_ready, k + 1)
                    pe.wait_ge(sl_ready, 1 + k)
                    mm(bank_m[:, 0:P], ones[:, :], diag[:, :], start=True, stop=True).then_inc(sl_done, 1)

            def layer(k, par):
                g = chunk_base(2) + NT + k
                pe.wait_ge(full_in[par], 32 * (k // 2 + 1))
                pe.wait_ge(ts_ready, 1 + k)
                for j in range(NT):
                    last = mm(bank_xa[:, 0:D], e_buf[par][:, j * P:(j + 1) * P], xs[:, j * W:j * W + D],
                              start=(j == 0), stop=(j == NT - 1))
                last.then_inc(ts_done, 1)
                pe.wait_ge(et_ready, k + 1)
                pe.wait_ge(comb_ready, k + 1)
                for j in range(NT):
                    last = mm(bank_l[par][:, 0:D + 1], kq[par][:, j * P:(j + 1) * P], hh[:, j * W:j * W + D + 1],
                              start=(j == 0), stop=(j == NT - 1))
                last.then_inc(att_done, 1)
                pe.wait_ge(ts_ready, 1 + k + 1)
                transpose_chunk(g, par, two_blocks(ts_st))
                pe.wait_ge(comb_ready, k + 2)
                use_chunk(g, par, [(bank_l[2][:, 0:W], c, wg_sb[:, c * W:(c + 1) * W], c == 0, c == 1)
                                   for c in range(2)])

            pe.wait_ge(hh_ready, 1 + NT)
            with pe.Fori(0, PAIRS) as pr:
                for u in range(2):
                    layer(2 * pr + u, u)

        @block.scalar
        def _(act):
            def copy(dst, src, scale=1.0):
                return nc.scalar.activation(dst, src, ACT.Copy, scale=scale)

            act.sem_inc(tr_ready, 2)

            def copy_chunk(g, par, width):
                act.wait_ge(tr_done, g + 1)
                act.wait_ge(tr_used, g + 1)
                copy(tr[par][:, 0:width], bank_t[par][:, 0:width]).then_inc(tr_ready, 1)

            def root(count):
                act.wait_ge(stats_ready, count)
                nc.scalar.activation(std[:, :], std[:, :], ACT.Sqrt).then_inc(std_ready, 1)
                act.wait_ge(rstd_ready, count)

            def norm_relu(dst, k):
                return nc.scalar.activation(dst, x1[:, bass.ds(k * D, D)], ACT.Relu,
                                            bias=shift[:, bass.ds(k, 1)], scale=rstd[:, bass.ds(k, 1)])

            act.wait_ge(w12_done, 1)
            for c in range(2):
                last = copy(wqk[:, c * P + DA:(c + 1) * P], bank_m[:, c * DA:(c + 1) * DA])
            last.then_inc(w12_ready, 1)
            root(1)
            with act.Fori(0, PAIRS) as pr:
                for u in range(2):
                    k = 2 * pr + u
                    norm_relu(stage[:, 5 * D:6 * D], k)
                    norm_relu(xs[:, bass.ds(k * W, D)], k).then_inc(h_ready, 1)
                    copy_chunk(k, u, 2 * P)
                    act.wait_ge(tr_used, k + 3)
                    copy(kq[0][:, bass.ds(k * P, P)], bank_m[:, 0:P]).then_inc(kq_ready, 1)

            def exps(step, k, par):
                n = step * NT + k
                for c in range(NL):
                    width = min(LC, N - c * LC)
                    act.wait_ge(l_done, NL * n + c + 1)
                    if c == 0:
                        act.wait_ge(a_ready, n)
                    copy(e_buf[par][:, c * LC:c * LC + width], bank_l[c % 3][:, 0:width]).then_inc(l_copied, 1)
                act.wait_ge(max_ready, n + 1)
                nc.scalar.activation(e_buf[par][:, 0:N], e_buf[par][:, 0:N], ACT.Exp, bias=neg_max[par][:, :],
                                     accum_out=z[par][:, :]).then_inc(exp_ready, 1)

            def out_of_a(step, k, par):
                n = step * NT + k
                g = chunk_base(step) + (8 if step == 0 else 10) * k
                for c in range(AC):
                    copy_chunk(g + c, c % 2, P * min(4, NT - 4 * c))
                act.wait_ge(tr_used, g + AC + 2)
                copy(stage[:, 5 * D:6 * D], bank_xa[:, 0:D], inv_kept[par][:, :])
                if step == 0:
                    copy(xa[:, bass.ds(k * W, D)], bank_xa[:, 0:D], inv_kept[par][:, :]).then_inc(xa_ready, 1)
                    copy_chunk(g + 7, 1, 2 * P)
                    act.wait_ge(tr_used, g + 10)
                    copy(kq[1][:, bass.ds(k * P, P)], bank_m[:, 0:P]).then_inc(kq_ready, 1)
                else:
                    copy(stage[:, 4 * D:5 * D], xa[:, bass.ds(k * W, D)]).then_inc(xa_ready, 1)
                    copy_chunk(g + 7, 1, 4 * P)
                    copy_chunk(g + 8, 0, 4 * P)
                    copy_chunk(g + 9, 1, 4 * P)

            def out_of_s(step, k):
                act.wait_ge(inv_ready, step * NT + k + 1)
                act.wait_ge(adj_used, 4 * k + 6 if step == 0 else 4 * NT + 2 * k + 4)
                if step == 0:
                    copy(fb[:, bass.ds(k * 2 * D, D)], bank_s[:, 0:D], inv_sum[:, 0:1])
                    copy(fb[:, bass.ds(k * 2 * D + D, D)], bank_s[:, 0:D], inv_sum[:, 1:2]).then_inc(s_ready, 1)
                else:
                    copy(stage[:, 0:2 * D], fb[:, bass.ds(k * 2 * D, 2 * D)])
                    copy(stage[:, 2 * D:3 * D], bank_s[:, 0:D], inv_sum[:, 0:1])
                    copy(stage[:, 3 * D:4 * D], bank_s[:, D:2 * D], inv_sum[:, 1:2]).then_inc(s_ready, 1)

            for step in range(2):
                def iteration(k, par, begins, ends):
                    if begins:
                        exps(step, k, par)
                    if ends:
                        out_of_a(step, k - 1, 1 - par)
                    if begins:
                        out_of_s(step, k)

                steps(act, iteration)

            root(2)
            root(3)
            with act.Fori(0, PAIRS) as pr:
                for u in range(2):
                    k = 2 * pr + u
                    g = chunk_base(2) + k
                    norm_relu(h_st, k)
                    norm_relu(xs[:, bass.ds(k * W, D)], k).then_inc(h_ready, 1)
                    copy_chunk(g, u, 2 * P)
                    act.wait_ge(tr_used, g + 3)
                    copy(hh[:, bass.ds(k * W, D)], bank_s[:, 0:D]).then_inc(hh_ready, 1)
                    act.wait_ge(sl_done, 1 + k + 1)
                    copy(slb[:, bass.ds(k * P, P)], bank_m[:, 0:P]).then_inc(sl_ready, 1)

            def layer(k, par, begins, ends):
                if begins:
                    act.wait_ge(score_ready, k + 1)
                    nc.scalar.activation(a_buf[:, :], a_buf[:, :], ACT.Exp).then_inc(score_exp, 1)
                if ends:
                    g = chunk_base(2) + NT + k - 1
                    copy_chunk(g, 1 - par, 2 * P)
                    act.wait_ge(gate_arg, k)
                    nc.scalar.activation(gate[:, 2:4], gate[:, 0:2], ACT.Exp, scale=-1.0).then_inc(gate_exp, 1)
                    act.wait_ge(comb_ready, k + 2)
                    nc.scalar.activation(work2, work2, ACT.Exp, scale=-1.0).then_inc(comb_exp, 1)
                if begins:
                    act.wait_ge(ts_done, k + 1)
                    copy(ts_st, bank_xa[:, 0:D]).then_inc(ts_ready, 1)

            steps(act, layer)

        @block.vector
        def _(dve):
            dve.sem_inc(comb_ready, 2)
            dve.wait_ge(const_ready, 1)

            def tile_stats(src, k):
                V.bn_stats(bst[:, :], src)
                dve.drain()
                V.bn_aggr(mv[:, :], bst[:, :])
                dve.drain()
                V.tensor_copy(mvs[:, bass.ds(2 * k, 2)], mv[:, :])

            def norms(count):
                both = mvs[:, :].rearrange("p (k t) -> p k t", t=2)
                dve.drain()
                V.tensor_scalar(std[:, :], both[:, :, 1], LN_EPS, None, ALU.add).then_inc(stats_ready, 1)
                dve.wait_ge(std_ready, count)
                V.reciprocal(rstd[:, :], std[:, :])
                dve.drain()
                V.scalar_tensor_tensor(out=shift[:, :], in0=both[:, :, 0], scalar=-1.0, in1=rstd[:, :],
                                       op0=ALU.mult, op1=ALU.mult).then_inc(rstd_ready, 1)

            dve.wait_ge(x_in, 16)
            with dve.Fori(0, NT) as k:
                tile_stats(x1[:, bass.ds(k * D, D)], k)
            norms(1)

            def mass_above(e, bound):
                V.scalar_tensor_tensor(out=junk[:, 0:N], in0=e[:, 0:N], scalar=bound, in1=e[:, 0:N],
                                       op0=ALU.is_ge, op1=ALU.mult, accum_out=mass[:, :])
                dve.drain()

            def search(par, halvings):
                e = e_buf[par]
                ratio = [SPAN ** (0.5 ** (i + 1)) for i in range(halvings)]
                V.tensor_scalar(tgt[:, 0:1], z[par][:, :], P_NUC, None, ALU.mult)
                V.tensor_scalar(tgt[:, 1:2], z[par][:, :], P_NUC, 1.0 - SLACK, ALU.mult, ALU.mult)
                V.tensor_scalar(lo[:, :], z[par][:, :], FLOOR, None, ALU.mult)
                V.tensor_scalar(mid[:, :], z[par][:, :], FLOOR, ratio[0], ALU.mult, ALU.mult)
                dve.drain()
                for i in range(halvings):
                    mass_above(e, mid[:, :])
                    V.tensor_scalar(inc[:, :], mass[:, :], tgt[:, 0:1], ratio[i] - 1.0, ALU.is_ge, ALU.mult)
                    dve.drain()
                    V.scalar_tensor_tensor(out=lo[:, :], in0=inc[:, :], scalar=1.0, in1=lo[:, :],
                                           op0=ALU.add, op1=ALU.mult)
                    dve.drain()
                    if i + 1 < halvings:
                        V.tensor_scalar(mid[:, :], lo[:, :], ratio[i + 1], None, ALU.mult)
                    else:
                        V.tensor_scalar(hi[:, :], lo[:, :], ratio[i] * (1.0 + 1e-6), None, ALU.mult)
                    dve.drain()

            def threshold(par):
                e = e_buf[par]
                V.scalar_tensor_tensor(out=a_buf[:, :], in0=e[:, :], scalar=hi[:, :], in1=e[:, :],
                                       op0=ALU.is_lt, op1=ALU.mult, accum_out=mass[:, :])
                dve.drain()
                V.max(top8[:, :], a_buf[:, :])
                V.tensor_scalar(above[:, :], mass[:, :], -1.0, z[par][:, :], ALU.mult, ALU.add)
                dve.drain()
                V.tensor_tensor_scan(cum8[:, :], top8[:, :], top8[:, :], above[:, :], ALU.add, ALU.max)
                dve.drain()
                V.tensor_tensor(cum8[:, :], cum8[:, :], top8[:, :], ALU.subtract)
                dve.drain()
                V.tensor_scalar(cum8[:, :], cum8[:, :], tgt[:, 0:1], 4.0, ALU.is_ge, ALU.mult)
                dve.drain()
                V.tensor_tensor(cum8[:, :], cum8[:, :], top8[:, :], ALU.add)
                dve.drain()
                V.tensor_reduce(tau[:, :], cum8[:, :], AX, ALU.min)
                dve.drain()
                V.scalar_tensor_tensor(out=a_buf[:, :], in0=e[:, :], scalar=tau[:, :], in1=e[:, :],
                                       op0=ALU.is_ge, op1=ALU.mult, accum_out=kept[:, :])
                dve.drain()

            def search_exactly(par):
                e = e_buf[par]
                first = SPAN ** (0.5 ** FAST_STEPS[0]) - 1.0
                V.tensor_scalar(wid[:, :], lo[:, :], first * 1.01, None, ALU.mult)
                dve.drain()
                with dve.Fori(0, EXACT_STEPS):
                    V.tensor_scalar(wid[:, :], wid[:, :], 0.5, None, ALU.mult)
                    dve.drain()
                    V.tensor_tensor(mid[:, :], lo[:, :], wid[:, :], ALU.add)
                    dve.drain()
                    mass_above(e, mid[:, :])
                    V.scalar_tensor_tensor(out=inc[:, :], in0=mass[:, :], scalar=tgt[:, 0:1], in1=wid[:, :],
                                           op0=ALU.is_ge, op1=ALU.mult)
                    dve.drain()
                    V.tensor_tensor(lo[:, :], lo[:, :], inc[:, :], ALU.add)
                    dve.drain()
                V.scalar_tensor_tensor(out=hi[:, :], in0=lo[:, :], scalar=1.0 + 2.0 ** -22, in1=wid[:, :],
                                       op0=ALU.mult, op1=ALU.add)
                dve.drain()
                with dve.Fori(0, EXACT_ROUNDS):
                    threshold(par)
                    V.tensor_scalar(bad[:, 0:1], kept[:, :], tgt[:, 1:2], None, ALU.is_lt)
                    V.tensor_tensor(inc[:, :], tau[:, :], hi[:, :], ALU.subtract)
                    dve.drain()
                    V.scalar_tensor_tensor(out=hi[:, :], in0=inc[:, :], scalar=bad[:, 0:1], in1=hi[:, :],
                                           op0=ALU.mult, op1=ALU.add)
                    dve.drain()

            def drop_ties(par):
                tie = e_buf[par]
                V.tensor_scalar(tie[:, :], a_buf[:, :], tau[:, :], None, ALU.is_equal)
                V.reciprocal(inc[:, :], tau[:, :])
                V.tensor_tensor(mid[:, :], tgt[:, 0:1], kept[:, :], ALU.subtract)
                dve.drain()
                V.tensor_tensor_scan(tie[:, :], tie[:, :], tie[:, :], 0.0, ALU.add, ALU.max)
                V.scalar_tensor_tensor(out=mid[:, :], in0=mid[:, :], scalar=inc[:, :], in1=ones[:, 0:1],
                                       op0=ALU.mult, op1=ALU.add)
                dve.drain()
                V.tensor_tensor(mid[:, :], mid[:, :], tie[:, NP - 1:NP], ALU.add)
                dve.drain()
                V.scalar_tensor_tensor(out=tie[:, :], in0=tie[:, :], scalar=mid[:, :], in1=a_buf[:, :],
                                       op0=ALU.is_ge, op1=ALU.mult)
                dve.drain()
                V.tensor_scalar(tie[:, :], tie[:, :], tau[:, :], tau[:, :], ALU.is_equal, ALU.mult)
                dve.drain()
                V.scalar_tensor_tensor(out=a_buf[:, :], in0=tie[:, :], scalar=-1.0, in1=a_buf[:, :],
                                       op0=ALU.mult, op1=ALU.add, accum_out=kept[:, :])
                dve.drain()

            def mask(step, k, par):
                g = chunk_base(step) + (8 if step == 0 else 10) * k
                dve.wait_ge(tr_done, g - (1 if step == 0 else 3))
                threshold(par)
                V.tensor_scalar(bad[:, 0:1], kept[:, :], tgt[:, 1:2], 100.0, ALU.is_lt, ALU.mult)
                V.tensor_scalar(bad[:, 1:2], kept[:, :], tau[:, :], tgt[:, 0:1], ALU.subtract, ALU.is_ge)
                dve.drain()
                V.tensor_tensor(flag[:, 0:1], bad[:, 0:1], bad[:, 1:2], ALU.add)
                dve.drain()
                V.transpose(flag_t[:, :], flag[:, :])
                dve.drain()
                V.tensor_reduce(flag_i[:, :], flag_t[:, :], AX, ALU.max)
                dve.drain()
                worst = [V.value_load(flag_i[32 * q:32 * q + 1, 0:1]) for q in range(4)]
                worst = worst[0] + worst[1] + worst[2] + worst[3]
                with dve.If(worst > 0):
                    with dve.If(worst > 99):
                        search_exactly(par)
                    drop_ties(par)
                V.reciprocal(inv_kept[par][:, :], kept[:, :]).then_inc(a_ready, 1)

            def inverse_sums(step, k):
                dve.wait_ge(s_ready, step * NT + k)
                if step == 0:
                    dve.wait_ge(adj_used, 4 * k + 6)
                    V.tensor_scalar(inv_sum[:, :], bank_s[:, D:D + 4:2], CLIP, None, ALU.max)
                    dve.drain()
                    V.reciprocal(inv_sum[:, :], inv_sum[:, :]).then_inc(inv_ready, 1)
                    dve.drain()
                    V.tensor_copy(inv_sums[:, bass.ds(2 * k, 2)], inv_sum[:, :])
                else:
                    V.tensor_copy(inv_sum[:, :], inv_sums[:, bass.ds(2 * k, 2)]).then_inc(inv_ready, 1)

            for step in range(2):
                def iteration(k, par, begins, ends):
                    n = step * NT + k
                    if begins:
                        dve.wait_ge(l_copied, NL * n + NL)
                        V.tensor_reduce(neg_max[par][:, :], e_buf[par][:, 0:N], AX, ALU.max,
                                        negate=True).then_inc(max_ready, 1)
                    if ends:
                        mask(step, k - 1, 1 - par)
                    if begins:
                        inverse_sums(step, k)
                        dve.wait_ge(exp_ready, n + 1)
                        search(par, FAST_STEPS[step])
                    if ends and step == 1:
                        dve.wait_ge(tr_used, chunk_base(1) + 10 * (k - 1) + 12)
                        y = xs[:, bass.ds((k - 1) * W, D)]
                        V.tensor_tensor(y, bank_m[:, 0:D], y, ALU.add).then_inc(y_ready, 1)

                steps(dve, iteration)

            dve.drain()
            with dve.Fori(0, NT) as k:
                tile_stats(xs[:, bass.ds(k * W, D)], k)
            norms(2)
            dve.wait_ge(x_in, 32)
            dve.wait_ge(late_in, 64)
            dve.drain()
            with dve.Fori(0, NT) as k:
                x1_k = x1[:, bass.ds(k * D, D)]
                V.tensor_scalar(work, xs[:, bass.ds(k * W, D)], rstd[:, bass.ds(k, 1)], shift[:, bass.ds(k, 1)],
                                ALU.mult, ALU.add)
                dve.drain()
                V.tensor_tensor(work, work, gamma, ALU.mult)
                dve.drain()
                V.tensor_tensor(work, work, beta, ALU.add)
                dve.drain()
                V.tensor_tensor(x1_k, x1_k, work, ALU.add)
                dve.drain()
                tile_stats(x1_k, k)
            norms(3)
            with dve.Fori(0, NT) as k:
                dve.drain()
                dve.wait_ge(hh_ready, 1 + k + 1)
                for i, (a, w) in enumerate(((a_left, work), (a_right, work2))):
                    V.scalar_tensor_tensor(out=w, in0=bank_s[:, 0:D], scalar=-1.0, in1=a, op0=ALU.mult,
                                           op1=ALU.mult, accum_out=n_s[:, i:i + 1])
                V.tensor_copy(hb[:, bass.ds(2 * k, 2)], bank_s[:, D:W]).then_inc(hh_read, 1)
                dve.drain()
                dve.wait_ge(sl_done, 1 + k)
                V.tensor_scalar(diag[:, :], ident[:, :], n_s[:, 0:1], None, ALU.mult).then_inc(diag_ready, 1)
                V.tensor_copy(n_sr[:, bass.ds(k, 1)], n_s[:, 1:2])

            def scores(k):
                grid = a_buf[:, :].rearrange("p (j c) -> p j c", c=P)
                V.tensor_tensor(grid, slb[:, bass.ds(k * P, P)].unsqueeze(1).to_broadcast([P, NT, P]),
                                n_sr[:, :].unsqueeze(2).to_broadcast([P, NT, P]), ALU.add)
                dve.drain()
                V.scalar_tensor_tensor(out=a_buf[:, :], in0=a_buf[:, :], scalar=0.01, in1=a_buf[:, :],
                                       op0=ALU.mult, op1=ALU.min).then_inc(score_ready, 1)

            def masked(k, par):
                dve.wait_ge(score_exp, k + 1)
                dve.wait_ge(full_in[par], 32 * (k // 2 + 1))
                dve.wait_ge(att_done, k + 1)
                V.scalar_tensor_tensor(out=kq[par][:, :], in0=e_buf[par][:, :], scalar=0.0, in1=a_buf[:, :],
                                       op0=ALU.not_equal, op1=ALU.mult).then_inc(et_ready, 1)

            def combine(k, par):
                att, gcn = bank_l[par], bank_l[2]
                dve.wait_ge(att_done, k + 3)
                dve.wait_ge(tr_used, chunk_base(2) + NT + k + 3)
                V.tensor_tensor(gate[:, 0:2], gcn[:, D:W], hb[:, bass.ds(2 * k, 2)], ALU.add)
                V.tensor_scalar(den[:, :], att[:, D:D + 1], 1e-5, None, ALU.add)
                dve.drain()
                V.tensor_tensor(gate[:, 0:2], gate[:, 0:2], gb_sb[:, :], ALU.add)
                V.tensor_tensor(work, gcn[:, 0:D], b_gcn, ALU.add)
                V.reciprocal(den[:, :], den[:, :])
                dve.drain()
                V.tensor_scalar(gate[:, 0:2], gate[:, 0:2], SIG_MIN, None, ALU.max).then_inc(gate_arg, 1)
                dve.wait_ge(gate_exp, k + 1)
                V.tensor_scalar(gate[:, 2:4], gate[:, 2:4], 1.0, None, ALU.add)
                dve.drain()
                V.reciprocal(gate[:, 2:4], gate[:, 2:4])
                dve.drain()
                V.tensor_tensor(den[:, :], den[:, :], gate[:, 2:3], ALU.mult)
                V.tensor_scalar(work, work, gate[:, 3:4], None, ALU.mult)
                dve.drain()
                V.scalar_tensor_tensor(out=work2, in0=att[:, 0:D], scalar=den[:, :], in1=work, op0=ALU.mult,
                                       op1=ALU.add)
                dve.drain()
                V.tensor_scalar(work2, work2, SIG_MIN, None, ALU.max).then_inc(comb_ready, 1)
                dve.wait_ge(comb_exp, k + 1)
                V.tensor_scalar(work2, work2, 1.0, None, ALU.add)
                dve.drain()
                V.reciprocal(work2, work2)
                dve.drain()
                dve.wait_ge(out_sent[par], 16 + 16 * (k // 2))
                V.tensor_tensor(out_st[par], work2, x1[:, bass.ds(k * D, D)], ALU.add).then_inc(out_ready, 1)

            def layer(k, par, begins, ends):
                dve.drain()
                if begins:
                    scores(k)
                if ends:
                    combine(k - 1, 1 - par)
                if begins:
                    masked(k, par)

            dve.wait_ge(sl_ready, 1 + NT)
            dve.drain()
            steps(dve, layer)


INPUTS = ("x", "adj_t", "adj_n", "w1t", "w2", "w3", "u_all", "wh", "wg", "rows", "gate_bias")


def kernel(**inputs):
    import concourse.bacc as bacc
    from concourse.bass_utils import run_bass_kernel_spmd

    a = {k: np.asarray(v) for k, v in inputs.items()}
    f32 = np.float32

    x = np.zeros((NP, D), f32)
    x[:N] = a["x"]
    adj = np.zeros((NP, NP), f32)
    adj[:N, :N] = a["adj"]
    blocks = adj.reshape(NT, P, NT, P)

    def halves(b):
        return np.ascontiguousarray(b.reshape(NT, P, 2, HALF * P).transpose(0, 2, 1, 3)).reshape(
            2 * NT, P, HALF * P)

    def by_feature(w):
        return np.ascontiguousarray(w.reshape(2, P, -1).transpose(1, 0, 2)).reshape(P, -1)

    u = [a["L0_gnn_U1"][0], a["L0_gnn_U2"][0], a["L0_gnn_U1"][1], a["L0_gnn_U2"][1],
         a["L0_gnn_U3"][0], a["L0_gnn_U3"][1]]
    wa, wb = a["L1_gnn_Wa"][0], a["L1_gnn_Wb"][0]
    rows = np.concatenate([a["L0_gnn_gamma"], a["L0_gnn_beta"], a["L1_gnn_a_sa"][0], a["L1_gnn_b_gcnb"]])
    gate_bias = np.concatenate([a["L1_gnn_ba"], a["L1_gnn_bb"]])
    arrays = {
        "x": np.ascontiguousarray(x.reshape(NT, P, D).transpose(1, 0, 2)).reshape(P, NT * D),
        "adj_t": halves(blocks.transpose(0, 3, 2, 1)),
        "adj_n": halves(blocks.transpose(2, 1, 0, 3)),
        "w1t": np.ascontiguousarray(a["L0_gnn_W1"].T),
        "w2": a["L0_gnn_W2"],
        "w3": a["L0_gnn_W3"],
        "u_all": np.concatenate([by_feature(w) for w in u], axis=1),
        "wh": by_feature(np.concatenate([a["L1_gnn_W_sa"], wa[D:, None], wb[D:, None]], axis=1)),
        "wg": by_feature(np.concatenate([a["L1_gnn_W_gcnb"], wa[:D, None], wb[:D, None]], axis=1)),
        "rows": np.ascontiguousarray(np.broadcast_to(rows, (P, rows.size))),
        "gate_bias": np.ascontiguousarray(np.broadcast_to(gate_bias, (P, 2))),
    }
    nc = bacc.Bacc("TRN2", target_bir_lowering=False, num_devices=1)
    args, fed = [], {}
    for name in INPUTS:
        fed[f"in_{name}"] = np.ascontiguousarray(arrays[name])
        args.append(nc.dram_tensor(f"in_{name}", arrays[name].shape, F32, kind="ExternalInput").ap())
    out = nc.dram_tensor("out", (N, D), F32, kind="ExternalOutput").ap()
    build(nc, *args, out)
    r = run_bass_kernel_spmd(nc, [fed], core_ids=[0])
    return r.results[0]["out"]
```

```python
from contextlib import ExitStack

import numpy as np
import concourse.bass as bass
from concourse import mybir

F32 = mybir.dt.float32
U8 = mybir.dt.uint8
I8 = mybir.dt.int8
I32 = mybir.dt.int32
ALU = mybir.AluOpType
ACT = mybir.ActivationFunctionType
AX = mybir.AxisListType.X

P = 128
N = 3327
NT = -(-N // P)
NP = NT * P
D = 256
DA = 64
W = D + 2
WH = D + 4
HALF = NT // 2
LC = 512
NL = -(-N // LC)
AC = -(-NT // 4)
PAIRS = NT // 2
P_NUC = 0.9
LN_EPS = 1e-5
CLIP = 1e-12
SIG_MIN = -87.0

FLOOR = (1.0 - P_NUC) * 0.999 / N
SPAN = 1.01 / FLOOR
COARSE = (3, 5)
HALVINGS = (7, 11)
MORE_ROUNDS = (1, 3)
EXACT_STEPS = 42
EXACT_ROUNDS = 4
FILL = ((8,) * 7, (4,) * 8)
ROW_MAX_AT = 1
TAKE = ((1,) * 10, (1,) * 11)
SLACK = 4e-6


def chunk_base(step):
    return (NT, NT + 8 * NT, NT + 18 * NT)[step]


def build(nc, x, adj_t, adj_n, w1t, w2, w3, u_all, wh, wg, rows, gate_bias, out):
    V = nc.vector
    with ExitStack() as ctx:
        def sb(name, shape, dt=F32):
            return ctx.enter_context(nc.sbuf_tensor(name, shape, dt))

        def ps(name, shape):
            return ctx.enter_context(nc.psum_tensor(name, shape, F32))

        def sem(name):
            return ctx.enter_context(nc.semaphore(name))

        xs = sb("xs", [P, NT * W])
        fb = sb("fb", [P, NT * 2 * D])
        xa = sb("xa", [P, NT * W])
        kq = [sb(f"kq{s}", [P, NP]) for s in range(2)]
        e_buf = [sb(f"e{i}", [P, NP]) for i in range(2)]
        a_buf = sb("a_buf", [P, NP])
        ring = sb("ring", [P, 2, HALF * P])
        tr = [sb(f"tr{i}", [P, 4 * P]) for i in range(2)]
        junk = sb("junk", [P, NP], U8)
        junk_act = sb("junk_act", [P, NP], I8)
        stage = sb("stage", [P, 6 * D])
        ident = sb("ident", [P, P])
        ones = sb("ones", [P, P])
        w_left = sb("w_left", [P, 2 * P])
        wqk = sb("wqk", [P, 2 * P])
        w1t_sb = sb("w1t_sb", [DA, D])
        w2_sb = sb("w2_sb", [DA, DA])
        q_st = [sb(f"q_st{i}", [DA, P]) for i in range(2)]
        neg_max = [sb(f"neg_max{i}", [P, 1]) for i in range(2)]
        z = [sb(f"z{i}", [P, 1]) for i in range(2)]
        inv_kept = [sb(f"inv_kept{i}", [P, 1]) for i in range(2)]
        inv_sum = sb("inv_sum", [P, 2])
        inv_sums = sb("inv_sums", [P, 2 * NT])
        tgt = sb("tgt", [P, 2])
        c_mid = [sb(f"c_mid{i}", [P, 1]) for i in range(2)]
        c_bias = sb("c_bias", [P, 1])
        c_off = sb("c_off", [P, 1])
        c_tgt = sb("c_tgt", [P, 1])
        c_relu = sb("c_relu", [P, 1])
        c_sign = sb("c_sign", [P, 1])
        c_sum = sb("c_sum", [P, 1])
        c_step = sb("c_step", [P, 1])
        lo = sb("lo", [P, 1])
        hi = sb("hi", [P, 1])
        mid = sb("mid", [P, 1])
        wid = sb("wid", [P, 1])
        inc = sb("inc", [P, 1])
        mass = sb("mass", [P, 1])
        above = sb("above", [P, 1])
        top8 = sb("top8", [P, 8])
        cum8 = sb("cum8", [P, 8])
        tau = sb("tau", [P, 1])
        kept = sb("kept", [P, 1])
        bad = sb("bad", [P, 2])
        flag = sb("flag", [P, 32])
        flag_t = sb("flag_t", [P, 32])
        flag_i = sb("flag_i", [P, 1], I32)
        bst = [sb(f"bst{i}", [P, 6]) for i in range(2)]
        mv = sb("mv", [P, 4])
        mvs = sb("mvs", [P, 2 * NT])
        std = sb("std", [P, NT])
        rstd = sb("rstd", [P, NT])
        shift = sb("shift", [P, NT])
        hb = sb("hb", [P, 3 * NT])
        n_w = sb("n_w", [P, 4])
        gate = sb("gate", [P, 4])
        den = sb("den", [P, 1])
        gb_sb = sb("gb_sb", [P, 2])
        x1 = fb[:, 0:NT * D]
        slb = fb[:, NT * D:NT * D + NP]
        hh = xa
        u_sb = kq[0][:, 0:6 * 2 * D]
        flat_ring = ring[:, :, :].rearrange("p a b -> p (a b)")
        wh_sb = flat_ring[:, 0:2 * WH]
        wg_sb = flat_ring[:, 2 * WH:2 * WH + 2 * W]
        rows_sb = flat_ring[:, 2 * WH + 2 * W:2 * WH + 2 * W + 5 * D]
        gamma, beta, a_left, a_right, b_gcn = (rows_sb[:, i * D:(i + 1) * D] for i in range(5))
        ts_st = stage[:, 0:D]
        work = stage[:, 2 * D:3 * D]
        work2 = stage[:, 3 * D:4 * D]
        out_st = [stage[:, 4 * D:5 * D], stage[:, 5 * D:6 * D]]

        bank_l = [ps(f"bank_l{i}", [P, LC]) for i in range(3)]
        bank_t = [ps(f"bank_t{i}", [P, LC]) for i in range(2)]
        bank_xa = ps("bank_xa", [P, LC])
        bank_s = ps("bank_s", [P, LC])
        bank_m = ps("bank_m", [P, LC])
        chunk_bank = [*bank_t, *bank_l, *bank_t, *bank_t[::-1], bank_t[1]]

        x_in = sem("x_in")
        w_in = sem("w_in")
        wqk_in = sem("wqk_in")
        u_in = sem("u_in")
        late_in = sem("late_in")
        const_ready = sem("const_ready")
        stats_ready = sem("stats_ready")
        std_ready = sem("std_ready")
        rstd_ready = sem("rstd_ready")
        h_ready = sem("h_ready")
        w12_done = sem("w12_done")
        w12_ready = sem("w12_ready")
        tr_done = sem("tr_done")
        tr_ready = sem("tr_ready")
        tr_used = sem("tr_used")
        kq_ready = sem("kq_ready")
        q_in = [sem(f"q_in{i}") for i in range(2)]
        l_done = sem("l_done")
        l_copied = sem("l_copied")
        max_ready = sem("max_ready")
        coarse_ready = sem("coarse_ready")
        a_ready = sem("a_ready")
        xa_ready = sem("xa_ready")
        adj_in = [sem(f"adj_in{i}") for i in range(2)]
        adj_used = sem("adj_used")
        inv_ready = sem("inv_ready")
        s_ready = sem("s_ready")
        y_ready = sem("y_ready")
        staged = sem("staged")
        w_left_ready = sem("w_left_ready")
        sl_ready = sem("sl_ready")
        hh_ready = sem("hh_ready")
        full_in = [sem(f"full_in{i}") for i in range(2)]
        score_ready = sem("score_ready")
        score_exp = sem("score_exp")
        et_ready = sem("et_ready")
        ts_done = sem("ts_done")
        ts_ready = sem("ts_ready")
        att_done = sem("att_done")
        gate_arg = sem("gate_arg")
        gate_exp = sem("gate_exp")
        comb_ready = sem("comb_ready")
        comb_exp = sem("comb_exp")
        out_ready = sem("out_ready")
        out_sent = [sem(f"out_sent{i}") for i in range(2)]

        block = ctx.enter_context(nc.Block())

        def steps(eng, iteration):
            iteration(0, 0, True, False, True)
            with eng.Fori(0, PAIRS - 1) as pr:
                iteration(2 * pr + 1, 1, True, True, True)
                iteration(2 * pr + 2, 0, True, True, True)
            iteration(NT - 1, 1, True, True, False)
            iteration(NT, 0, False, True, False)

        @block.sync
        def _(sp):
            for u in range(2):
                sp.sem_inc(out_sent[u], 16)
            for from_one in (kq_ready, xa_ready, a_ready, y_ready, hh_ready, sl_ready, ts_ready):
                sp.sem_inc(from_one, 1)
            sp.dma_start(x1, x).then_inc(x_in, 16)
            sp.dma_start(w1t_sb[:, :], w1t).then_inc(w_in, 16)
            sp.dma_start(w2_sb[:, :], w2).then_inc(w_in, 16)
            for c in range(2):
                sp.dma_start(wqk[:, c * P:c * P + DA], w3[c * P:(c + 1) * P, :]).then_inc(wqk_in, 16)

            def load_q(step, k, par):
                sp.dma_start(q_st[par][:, :], kq[step][DA:P, bass.ds(k * P, P)]).then_inc(q_in[par], 16)

            def load_adj(src, k, half, piece):
                sp.wait_ge(adj_used, piece + 1)
                sp.dma_start(ring[:, half, :], src[bass.ds(2 * k + half, 1), :, :].rearrange(
                    "a p n -> (a p) n")).then_inc(adj_in[half], 16)

            def pieces(step, k):
                if step == 0:
                    for j, src in enumerate((adj_t, adj_t, adj_n, adj_n)):
                        load_adj(src, k, j % 2, 4 * k + j)
                else:
                    for half in range(2):
                        load_adj(adj_t, k, half, 4 * NT + 2 * k + half)

            for step in range(2):
                sp.wait_ge(kq_ready, 1 + (step + 1) * NT)
                load_q(step, 0, 0)
                load_q(step, 1, 1)
                if step == 1:
                    sp.wait_ge(l_done, NL * NT)
                    sp.dma_start(u_sb, u_all).then_inc(u_in, 16)
                with sp.Fori(0, PAIRS - 1) as pr:
                    for u in range(2):
                        sp.wait_ge(l_done, NL * (step * NT + 2 * pr + u + 1))
                        load_q(step, 2 * pr + u + 2, u)
                        pieces(step, 2 * pr + u)
                for u in range(2):
                    pieces(step, NT - 2 + u)
            sp.wait_ge(adj_used, 6 * NT + 2)
            sp.wait_ge(y_ready, 1 + NT)
            sp.dma_start(wh_sb, wh).then_inc(late_in, 16)
            sp.dma_start(wg_sb, wg).then_inc(late_in, 16)
            sp.dma_start(rows_sb, rows).then_inc(late_in, 16)
            sp.dma_start(gb_sb[:, :], gate_bias).then_inc(late_in, 16)
            sp.dma_start(x1, x).then_inc(x_in, 16)

            def load_full(k, par):
                for half in range(2):
                    sp.dma_start(e_buf[par][:, half * HALF * P:(half + 1) * HALF * P],
                                 adj_t[bass.ds(2 * k + half, 1), :, :].rearrange("a p n -> (a p) n")
                                 ).then_inc(full_in[par], 16)

            def store(k, par):
                sp.wait_ge(out_ready, k + 1)
                sp.dma_start(out[bass.ds(k * P, P), :], out_st[par]).then_inc(out_sent[par], 16)

            sp.wait_ge(a_ready, 1 + 2 * NT)
            sp.wait_ge(tr_ready, chunk_base(2) + 2)
            load_full(0, 0)
            load_full(1, 1)
            with sp.Fori(0, PAIRS - 1) as pr:
                for u in range(2):
                    sp.wait_ge(et_ready, 2 * pr + u + 1)
                    sp.wait_ge(ts_done, 2 * pr + u + 1)
                    load_full(2 * pr + u + 2, u)
                    store(2 * pr + u, u)
            store(NT - 2, 0)
            sp.wait_ge(out_ready, NT)
            sp.dma_start(out[(NT - 1) * P:N, :], out_st[1][0:N - (NT - 1) * P, :]).then_inc(out_sent[1], 16)
            for u in range(2):
                sp.wait_ge(out_sent[u], 16 + 16 * PAIRS)

        @block.gpsimd
        def _(pool):
            nc.gpsimd.memset(ident[:, :], 0.0)
            nc.gpsimd.memset(ones[:, :], 1.0)
            nc.gpsimd.memset(flag[:, :], 0.0)
            for e in e_buf:
                nc.gpsimd.memset(e[:, N:NP], 0.0)
            for rows_with_ones in (xs, xa):
                cols = rows_with_ones[:, :].rearrange("p (k w) -> p k w", w=W)
                nc.gpsimd.memset(cols[:, :, D:W], 1.0)
            pool.drain()
            nc.gpsimd.affine_select(out=ident[:, :], in_=ident[:, :], compare_op=ALU.not_equal, fill=1.0,
                                    base=0, pattern=[[-1, P]], channel_multiplier=1)
            pool.drain().then_inc(const_ready, 1)
            pool.wait_ge(s_ready, NT)
            pool.wait_ge(xa_ready, 1 + NT)
            with pool.Fori(0, NT) as k:
                pool.wait_ge(tr_done, chunk_base(1) + 10 * k)
                nc.gpsimd.tensor_copy(stage[:, 0:2 * D], fb[:, bass.ds(k * 2 * D, 2 * D)])
                nc.gpsimd.tensor_copy(stage[:, 4 * D:5 * D], xa[:, bass.ds(k * W, D)])
                pool.drain().then_inc(staged, 1)

        @block.tensor
        def _(pe):
            mm = nc.tensor.matmul
            pe.sem_inc(adj_used, 2)
            pe.sem_inc(tr_used, 2)
            pe.sem_inc(att_done, 2)
            pe.wait_ge(const_ready, 1)
            pe.wait_ge(w_in, 32)
            for c in range(2):
                last = mm(bank_m[:, c * DA:(c + 1) * DA], w1t_sb[:, c * P:(c + 1) * P], w2_sb[:, :],
                          start=True, stop=True)
            last.then_inc(w12_done, 1)
            pe.wait_ge(w12_ready, 1)
            pe.wait_ge(wqk_in, 32)

            def transpose_blocks(bank, blocks):
                for b, source in enumerate(blocks):
                    last = nc.tensor.transpose(bank[:, b * P:(b + 1) * P], source, ident[:, :])
                last.then_inc(tr_done, 1)

            def transpose_chunk(g, par, blocks):
                pe.wait_ge(tr_ready, g + 1)
                transpose_blocks(bank_t[par], blocks)

            def use_chunk(g, par, products):
                pe.wait_ge(tr_ready, g + 3)
                for o, b, other, start, stop in products:
                    last = mm(o, tr[par][:, b * P:(b + 1) * P], other, start=start, stop=stop)
                last.then_inc(tr_used, 1)

            def two_blocks(rows):
                return rows[:, 0:P], rows[:, P:2 * P]

            def project_kq(g, par, m):
                pe.wait_ge(tr_ready, g + 3)
                pe.wait_ge(kq_ready, 1 + m)
                for c in range(2):
                    last = mm(bank_m[:, 0:P], wqk[:, c * P:(c + 1) * P], tr[par][:, c * P:(c + 1) * P],
                              start=(c == 0), stop=(c == 1))
                last.then_inc(tr_used, 1)

            def first_kq(k, par, begins, ends, ahead):
                if begins:
                    pe.wait_ge(h_ready, k + 1)
                    transpose_chunk(k, par, two_blocks(stage[:, (4 + par) * D:(5 + par) * D]))
                if ends:
                    project_kq(k - 1, 1 - par, k - 1)

            steps(pe, first_kq)

            def logits(step, k, par):
                n = step * NT + k
                pe.wait_ge(q_in[par], 16 * (step * PAIRS + k // 2 + 1))
                for c in range(NL):
                    width = min(LC, N - c * LC)
                    pe.wait_ge(l_copied, NL * n + c - 2 if c >= 3 else NL * n)
                    mm(bank_l[c % 3][:, 0:width], q_st[par][:, :], kq[step][0:DA, c * LC:c * LC + width],
                       start=True, stop=True).then_inc(l_done, 1)

            def s_product(step, k):
                pe.wait_ge(s_ready, step * NT + k)
                src, row, width = (xs, W, D + 1) if step == 0 else (fb, 2 * D, 2 * D)
                mm(bank_s[:, 0:width], ident[:, :], src[:, bass.ds(k * row, width)], start=True, stop=False)
                yield
                for half in range(2):
                    pe.wait_ge(adj_in[half], 16 * (2 * k + 1 if step == 0 else 2 * NT + k + 1))
                    for b in range(HALF):
                        j = half * HALF + b
                        last = mm(bank_s[:, 0:width], ring[:, half, b * P:(b + 1) * P],
                                  src[:, j * row:j * row + width], start=False, stop=(j == NT - 1))
                        if b == HALF - 1:
                            last.then_inc(adj_used, 1)
                        yield
                if step == 0:
                    sums = bank_s[:, D + 4:D + 4 + P]
                    mm(sums, ones[:, :], ident[:, :], start=True, stop=False)
                    yield
                    for half in range(2):
                        pe.wait_ge(adj_in[half], 16 * (2 * k + 2))
                        for b in range(HALF):
                            last = mm(sums, ones[:, :], ring[:, half, b * P:(b + 1) * P],
                                      start=False, stop=(half == 1 and b == HALF - 1))
                            if b == HALF - 1:
                                last.then_inc(adj_used, 1)
                            yield

            def some(work, n):
                for _ in range(n):
                    next(work, None)

            def a_product(step, k, between, n_between, logits_out):
                n = step * NT + k
                g = chunk_base(step) + (8 if step == 0 else 10) * k
                src = xs if step == 0 else xa
                pe.wait_ge(a_ready, 1 + n + 1)

                def product(c):
                    if c == 0:
                        pe.wait_ge(xa_ready, 1 + n)
                    use_chunk(g + c, c % 2, [(bank_xa[:, 0:D], j % 4, src[:, j * W:j * W + D],
                                              j == 0, j == NT - 1) for j in range(4 * c, min(4 * c + 4, NT))])

                def transpose_a(c):
                    transpose_blocks(chunk_bank[c], [a_buf[:, j * P:(j + 1) * P]
                                                     for j in range(4 * c, min(4 * c + 4, NT))])

                pe.wait_ge(tr_ready, g + 2)
                transpose_a(0)
                transpose_a(1)
                pe.wait_ge(l_copied, logits_out)
                for c in range(2, 5):
                    transpose_a(c)
                for c in range(AC):
                    if c < 2:
                        pe.wait_ge(tr_ready, g + c + 3)
                        transpose_a(5 + c)
                    product(c)
                    some(between, n_between[c])
                if step == 0:
                    pe.wait_ge(xa_ready, 1 + n + 1)
                    transpose_chunk(g + 7, 1, two_blocks(stage[:, 5 * D:6 * D]))
                    project_kq(g + 7, 1, NT + k)
                    return

                def four_blocks(c):
                    return [stage[:, (4 * c + b) * P:(4 * c + b + 1) * P] for b in range(4)]

                def z_product(c):
                    use_chunk(g + 7 + c, (7 + c) % 2,
                              [(bank_m[:, 0:D], b, u_sb[:, (4 * c + b) * D:(4 * c + b + 1) * D],
                                c == 0 and b == 0, c == 2 and b == 3) for b in range(4)])

                pe.wait_ge(staged, k + 1)
                pe.wait_ge(s_ready, n + 1)
                pe.wait_ge(u_in, 16)
                pe.wait_ge(kq_ready, 1 + 2 * NT)
                pe.wait_ge(y_ready, 1 + k)
                transpose_chunk(g + 7, 1, four_blocks(0))
                transpose_chunk(g + 8, 0, four_blocks(1))
                z_product(0)
                some(between, n_between[AC])
                pe.wait_ge(xa_ready, 1 + n + 1)
                transpose_chunk(g + 9, 1, four_blocks(2))
                z_product(1)
                z_product(2)

            for step in range(2):
                def iteration(k, par, begins, ends, ahead):
                    between = s_product(step, k) if begins else iter(())
                    if ahead:
                        logits(step, k + 1, 1 - par)
                    if ends:
                        a_product(step, k - 1, between, FILL[step],
                                  NL * (step * NT + (k + 2 if ahead else NT)))
                    for _ in between:
                        pass

                logits(step, 0, 0)
                steps(pe, iteration)

            pe.wait_ge(late_in, 64)
            pe.wait_ge(w_left_ready, 1)

            def h_product(k, par, begins, ends, ahead):
                if begins:
                    pe.wait_ge(h_ready, NT + k + 1)
                    transpose_chunk(chunk_base(2) + k, par, two_blocks(stage[:, (4 + par) * D:(5 + par) * D]))
                if ends:
                    t = tr[1 - par]
                    pe.wait_ge(tr_ready, chunk_base(2) + k - 1 + 3)
                    pe.wait_ge(hh_ready, 1 + k - 1)
                    for c in range(2):
                        mm(bank_s[:, 0:WH], t[:, c * P:(c + 1) * P], wh_sb[:, c * WH:(c + 1) * WH],
                           start=(c == 0), stop=(c == 1))
                    for c in range(2):
                        last = mm(bank_m[:, 0:P], w_left[:, c * P:(c + 1) * P], t[:, c * P:(c + 1) * P],
                                  start=(c == 0), stop=(c == 1))
                    last.then_inc(tr_used, 1)

            steps(pe, h_product)

            def layer(k, par):
                g = chunk_base(2) + NT + k
                pe.wait_ge(full_in[par], 32 * (k // 2 + 1))
                pe.wait_ge(ts_ready, 1 + k)
                for j in range(NT):
                    last = mm(bank_xa[:, 0:D], e_buf[par][:, j * P:(j + 1) * P], xs[:, j * W:j * W + D],
                              start=(j == 0), stop=(j == NT - 1))
                last.then_inc(ts_done, 1)
                pe.wait_ge(et_ready, k + 1)
                pe.wait_ge(comb_ready, k + 1)
                for j in range(NT):
                    last = mm(bank_l[par][:, 0:D + 1], kq[par][:, j * P:(j + 1) * P], hh[:, j * W:j * W + D + 1],
                              start=(j == 0), stop=(j == NT - 1))
                last.then_inc(att_done, 1)
                pe.wait_ge(ts_ready, 1 + k + 1)
                transpose_chunk(g, par, two_blocks(ts_st))
                pe.wait_ge(comb_ready, k + 2)
                use_chunk(g, par, [(bank_l[2][:, 0:W], c, wg_sb[:, c * W:(c + 1) * W], c == 0, c == 1)
                                   for c in range(2)])

            pe.wait_ge(hh_ready, 1 + NT)
            with pe.Fori(0, PAIRS) as pr:
                for u in range(2):
                    layer(2 * pr + u, u)

        @block.scalar
        def _(act):
            def copy(dst, src, scale=1.0):
                return nc.scalar.activation(dst, src, ACT.Copy, scale=scale)

            act.sem_inc(tr_ready, 2)

            def copy_chunk(g, par, width, bank=None):
                act.wait_ge(tr_done, g + 1)
                act.wait_ge(tr_used, g + 1)
                copy(tr[par][:, 0:width], (bank or bank_t[par])[:, 0:width]).then_inc(tr_ready, 1)

            def root(count):
                act.wait_ge(stats_ready, count)
                nc.scalar.activation(std[:, :], std[:, :], ACT.Sqrt).then_inc(std_ready, 1)
                act.wait_ge(rstd_ready, count)

            def norm_relu(dst, k):
                return nc.scalar.activation(dst, x1[:, bass.ds(k * D, D)], ACT.Relu,
                                            bias=shift[:, bass.ds(k, 1)], scale=rstd[:, bass.ds(k, 1)])

            act.wait_ge(w12_done, 1)
            for c in range(2):
                last = copy(wqk[:, c * P + DA:(c + 1) * P], bank_m[:, c * DA:(c + 1) * DA])
            last.then_inc(w12_ready, 1)
            root(1)

            def first_kq(k, par, begins, ends, ahead):
                if begins:
                    act.wait_ge(tr_ready, k + 1)
                    norm_relu(stage[:, (4 + par) * D:(5 + par) * D], k).then_inc(h_ready, 1)
                if ends:
                    act.wait_ge(tr_used, k + 2)
                    copy(kq[0][:, bass.ds((k - 1) * P, P)], bank_m[:, 0:P]).then_inc(kq_ready, 1)

            steps(act, first_kq)

            def chunk_of(step, k):
                return chunk_base(step) + (8 if step == 0 else 10) * k

            def copy_logits(step, k, par):
                n = step * NT + k
                for c in range(NL):
                    width = min(LC, N - c * LC)
                    act.wait_ge(l_done, NL * n + c + 1)
                    if c == 0:
                        act.wait_ge(a_ready, n)
                    copy(e_buf[par][:, c * LC:c * LC + width], bank_l[c % 3][:, 0:width]).then_inc(l_copied, 1)

            def exps(step, k, par):
                act.drain()
                act.wait_ge(max_ready, step * NT + k + 1)
                nc.scalar.activation(e_buf[par][:, 0:N], e_buf[par][:, 0:N], ACT.Exp, bias=neg_max[par][:, :],
                                     accum_out=z[par][:, :])
                act.drain()

            def coarse_start(par):
                copy(c_tgt[:, :], z[par][:, :], -2.0 * P_NUC)
                copy(c_mid[par][:, :], z[par][:, :], FLOOR * SPAN ** 0.5)

            def coarse_sums(par):
                act.drain()
                copy(c_bias[:, :], c_mid[par][:, :], -2.0)
                nc.scalar.activation(c_off[:, :], c_mid[par][:, :], ACT.Identity, scale=float(N), bias=c_tgt[:, :])
                act.drain()
                nc.scalar.activation(junk_act[:, 0:N], e_buf[par][:, 0:N], ACT.Relu, scale=2.0, bias=c_bias[:, :],
                                     accum_out=c_relu[:, :])

            def coarse_count(par):
                act.drain()
                nc.scalar.activation(junk_act[:, 0:N], e_buf[par][:, 0:N], ACT.Sign, scale=2.0, bias=c_bias[:, :],
                                     accum_out=c_sign[:, :])

            def coarse_move(par, level, last):
                act.drain()
                nc.scalar.activation(c_sum[:, :], c_sign[:, :], ACT.Identity, scale=c_mid[par][:, :],
                                     bias=c_relu[:, :])
                act.drain()
                nc.scalar.activation(c_step[:, :], c_sum[:, :], ACT.Sign, bias=c_off[:, :])
                act.drain()
                nc.scalar.activation(c_step[:, :], c_step[:, :], ACT.Exp,
                                     scale=float(np.log(SPAN) * 0.5 ** (level + 2)))
                act.drain()
                moved = copy(c_mid[par][:, :], c_mid[par][:, :], c_step[:, :])
                if last:
                    moved.then_inc(coarse_ready, 1)

            def ahead_parts(step, k, par):
                parts = [lambda: (exps(step, k, par), coarse_start(par))]
                for level in range(COARSE[step]):
                    parts += [lambda: coarse_sums(par),
                              lambda level=level: (coarse_count(par),
                                                   coarse_move(par, level, level == COARSE[step] - 1))]
                return parts

            def out_of_s(step, k):
                act.wait_ge(inv_ready, step * NT + k + 1)
                act.wait_ge(adj_used, 4 * k + 6 if step == 0 else 4 * NT + 2 * k + 4)
                if step == 0:
                    copy(fb[:, bass.ds(k * 2 * D, D)], bank_s[:, 0:D], inv_sum[:, 0:1])
                    copy(fb[:, bass.ds(k * 2 * D + D, D)], bank_s[:, 0:D], inv_sum[:, 1:2]).then_inc(s_ready, 1)
                else:
                    copy(stage[:, 2 * D:3 * D], bank_s[:, 0:D], inv_sum[:, 0:1])
                    copy(stage[:, 3 * D:4 * D], bank_s[:, D:2 * D], inv_sum[:, 1:2]).then_inc(s_ready, 1)

            def end_parts(step, k, par):
                g = chunk_of(step, k)

                def xa_out():
                    act.wait_ge(tr_used, g + AC + 2)
                    if step == 0:
                        copy(xa[:, bass.ds(k * W, D)], bank_xa[:, 0:D], inv_kept[par][:, :])
                    copy(stage[:, 5 * D:6 * D], bank_xa[:, 0:D], inv_kept[par][:, :]).then_inc(xa_ready, 1)

                def kq_out():
                    act.wait_ge(tr_used, g + 10)
                    copy(kq[1][:, bass.ds(k * P, P)], bank_m[:, 0:P]).then_inc(kq_ready, 1)

                parts = [lambda c=c: copy_chunk(g + c, c % 2, P * min(4, NT - 4 * c), chunk_bank[c])
                         for c in range(AC)]
                if step == 0:
                    return parts + [xa_out, lambda: copy_chunk(g + 7, 1, 2 * P), kq_out]
                return parts + [xa_out] + [lambda c=c: copy_chunk(g + c, c % 2, 4 * P) for c in (7, 8, 9)]

            for step in range(2):
                def iteration(k, par, begins, ends, ahead):
                    coarse = ahead_parts(step, k + 1, 1 - par) if ahead else []
                    ending = end_parts(step, k - 1, 1 - par) if ends else []
                    if ahead:
                        copy_logits(step, k + 1, 1 - par)
                    if ends:
                        out_of_s(step, k - 1)
                    for take in TAKE[step]:
                        for part in ending[:take]:
                            part()
                        ending = ending[take:]
                        for part in coarse[:1]:
                            part()
                        coarse = coarse[1:]
                    for part in ending + coarse:
                        part()

                copy_logits(step, 0, 0)
                exps(step, 0, 0)
                copy(c_mid[0][:, :], z[0][:, :], FLOOR * SPAN ** 0.5).then_inc(coarse_ready, 1)
                steps(act, iteration)

            root(2)
            root(3)

            def h_product(k, par, begins, ends, ahead):
                if begins:
                    act.wait_ge(tr_ready, chunk_base(2) + k + 1)
                    norm_relu(stage[:, (4 + par) * D:(5 + par) * D], k).then_inc(h_ready, 1)
                if ends:
                    act.wait_ge(tr_used, chunk_base(2) + k + 2)
                    copy(hh[:, bass.ds((k - 1) * W, D)], bank_s[:, 0:D])
                    copy(hb[:, bass.ds(3 * (k - 1), 3)], bank_s[:, D:D + 3])
                    copy(slb[:, bass.ds((k - 1) * P, P)], bank_m[:, 0:P]).then_inc(hh_ready, 1)

            steps(act, h_product)
            act.drain().then_inc(sl_ready, 1)

            def score_exps(k):
                act.wait_ge(score_ready, k + 1)
                nc.scalar.activation(a_buf[:, :], a_buf[:, :], ACT.Exp).then_inc(score_exp, 1)

            def layer(k, par, begins, ends, ahead):
                if ahead:
                    score_exps(k + 1)
                if ends:
                    copy_chunk(chunk_base(2) + NT + k - 1, 1 - par, 2 * P)
                    act.wait_ge(gate_arg, k)
                    nc.scalar.activation(gate[:, 2:4], gate[:, 0:2], ACT.Exp, scale=-1.0).then_inc(gate_exp, 1)
                    act.wait_ge(comb_ready, k + 2)
                    nc.scalar.activation(work2, work2, ACT.Exp, scale=-1.0).then_inc(comb_exp, 1)
                if begins:
                    act.wait_ge(ts_done, k + 1)
                    copy(ts_st, bank_xa[:, 0:D]).then_inc(ts_ready, 1)

            score_exps(0)
            steps(act, layer)

        @block.vector
        def _(dve):
            dve.sem_inc(comb_ready, 2)
            dve.wait_ge(const_ready, 1)

            def pair_stats(src, pr):
                for u in range(2):
                    V.bn_stats(bst[u][:, :], src(2 * pr + u))
                dve.drain()
                for u in range(2):
                    V.bn_aggr(mv[:, 2 * u:2 * u + 2], bst[u][:, :])
                dve.drain()
                V.tensor_copy(mvs[:, bass.ds(4 * pr, 4)], mv[:, :])

            def copy_rows(first, h_first):
                with dve.Fori(0, PAIRS) as pr:
                    for u in range(2):
                        k = 2 * pr + u
                        dve.wait_ge(h_ready, h_first + k + 1)
                        V.tensor_copy(xs[:, bass.ds(k * W, D)], stage[:, (4 + u) * D:(5 + u) * D])
                        dve.wait_ge(tr_done, first + k + 1)
                        dve.wait_ge(tr_used, first + k + 1)
                        V.tensor_copy(tr[u][:, 0:2 * P], bank_t[u][:, 0:2 * P])
                        dve.drain().then_inc(tr_ready, 1)

            def norms(count):
                both = mvs[:, :].rearrange("p (k t) -> p k t", t=2)
                dve.drain()
                V.tensor_scalar(std[:, :], both[:, :, 1], LN_EPS, None, ALU.add).then_inc(stats_ready, 1)
                dve.wait_ge(std_ready, count)
                V.reciprocal(rstd[:, :], std[:, :])
                dve.drain()
                V.scalar_tensor_tensor(out=shift[:, :], in0=both[:, :, 0], scalar=-1.0, in1=rstd[:, :],
                                       op0=ALU.mult, op1=ALU.mult).then_inc(rstd_ready, 1)

            dve.wait_ge(x_in, 16)
            with dve.Fori(0, PAIRS) as pr:
                pair_stats(lambda k: x1[:, bass.ds(k * D, D)], pr)
            norms(1)
            copy_rows(0, 0)

            def mass_above(e, bound):
                V.scalar_tensor_tensor(out=junk[:, 0:N], in0=e[:, 0:N], scalar=bound, in1=e[:, 0:N],
                                       op0=ALU.is_ge, op1=ALU.mult, accum_out=mass[:, :])
                dve.drain()

            def targets(par):
                V.tensor_scalar(tgt[:, 0:1], z[par][:, :], P_NUC, None, ALU.mult)
                V.tensor_scalar(tgt[:, 1:2], z[par][:, :], P_NUC, 1.0 - SLACK, ALU.mult, ALU.mult)
                V.tensor_copy(mid[:, :], c_mid[par][:, :])
                dve.drain()

            def search(par, levels, last):
                for i in levels:
                    mass_above(e_buf[par], mid[:, :])
                    ratio = SPAN ** (0.5 ** (i + 1 if i == last else i + 2))
                    down = 1.0 if i == last else 1.0 / ratio
                    V.tensor_scalar(inc[:, :], mass[:, :], tgt[:, 0:1], ratio - down, ALU.is_ge, ALU.mult)
                    dve.drain()
                    V.scalar_tensor_tensor(out=hi[:, :] if i == last else mid[:, :], in0=inc[:, :], scalar=down,
                                           in1=mid[:, :], op0=ALU.add, op1=ALU.mult)
                    dve.drain()

            def threshold(par):
                e = e_buf[par]
                V.scalar_tensor_tensor(out=a_buf[:, :], in0=e[:, :], scalar=hi[:, :], in1=e[:, :],
                                       op0=ALU.is_lt, op1=ALU.mult, accum_out=mass[:, :])
                dve.drain()
                V.max(top8[:, :], a_buf[:, :])
                V.tensor_scalar(above[:, :], mass[:, :], -1.0, z[par][:, :], ALU.mult, ALU.add)
                dve.drain()
                V.tensor_tensor(above[:, :], above[:, :], tgt[:, 1:2], ALU.min)
                dve.drain()
                V.tensor_tensor_scan(cum8[:, :], top8[:, :], top8[:, :], above[:, :], ALU.add, ALU.max)
                dve.drain()
                V.tensor_tensor(cum8[:, :], cum8[:, :], top8[:, :], ALU.subtract)
                dve.drain()
                V.tensor_scalar(cum8[:, :], cum8[:, :], tgt[:, 0:1], 4.0, ALU.is_ge, ALU.mult)
                dve.drain()
                V.tensor_tensor(cum8[:, :], cum8[:, :], top8[:, :], ALU.add)
                dve.drain()
                V.tensor_reduce(tau[:, :], cum8[:, :], AX, ALU.min)
                dve.drain()
                V.scalar_tensor_tensor(out=a_buf[:, :], in0=e[:, :], scalar=tau[:, :], in1=e[:, :],
                                       op0=ALU.is_ge, op1=ALU.mult, accum_out=kept[:, :])
                dve.drain()

            def more_candidates(par, rounds):
                with dve.Fori(0, rounds):
                    V.tensor_scalar(bad[:, 0:1], kept[:, :], tgt[:, 1:2], None, ALU.is_lt)
                    V.tensor_tensor(inc[:, :], tau[:, :], hi[:, :], ALU.subtract)
                    dve.drain()
                    V.scalar_tensor_tensor(out=hi[:, :], in0=inc[:, :], scalar=bad[:, 0:1], in1=hi[:, :],
                                           op0=ALU.mult, op1=ALU.add)
                    dve.drain()
                    threshold(par)

            def search_exactly(par):
                e = e_buf[par]
                V.tensor_scalar(lo[:, :], z[par][:, :], FLOOR, None, ALU.mult)
                V.memset(wid[:, :], 1.01)
                dve.drain()
                with dve.Fori(0, EXACT_STEPS):
                    V.tensor_scalar(wid[:, :], wid[:, :], 0.5, None, ALU.mult)
                    dve.drain()
                    V.tensor_tensor(mid[:, :], lo[:, :], wid[:, :], ALU.add)
                    dve.drain()
                    mass_above(e, mid[:, :])
                    V.scalar_tensor_tensor(out=inc[:, :], in0=mass[:, :], scalar=tgt[:, 0:1], in1=wid[:, :],
                                           op0=ALU.is_ge, op1=ALU.mult)
                    dve.drain()
                    V.tensor_tensor(lo[:, :], lo[:, :], inc[:, :], ALU.add)
                    dve.drain()
                V.scalar_tensor_tensor(out=hi[:, :], in0=lo[:, :], scalar=1.0 + 2.0 ** -22, in1=wid[:, :],
                                       op0=ALU.mult, op1=ALU.add)
                dve.drain()
                threshold(par)
                more_candidates(par, EXACT_ROUNDS)

            def drop_ties(par):
                tie = e_buf[par]
                V.tensor_scalar(junk[:, :], a_buf[:, :], tau[:, :], None, ALU.is_equal)
                V.reciprocal(inc[:, :], tau[:, :])
                V.tensor_tensor(mid[:, :], tgt[:, 0:1], kept[:, :], ALU.subtract)
                V.tensor_scalar(lo[:, :], tau[:, :], -1.0, None, ALU.mult)
                dve.drain()
                V.tensor_tensor_scan(tie[:, :], junk[:, :], junk[:, :], 0.0, ALU.add, ALU.max)
                V.scalar_tensor_tensor(out=mid[:, :], in0=mid[:, :], scalar=inc[:, :], in1=ones[:, 0:1],
                                       op0=ALU.mult, op1=ALU.add)
                dve.drain()
                V.tensor_tensor(mid[:, :], mid[:, :], tie[:, NP - 1:NP], ALU.add)
                dve.drain()
                V.scalar_tensor_tensor(out=tie[:, :], in0=tie[:, :], scalar=mid[:, :], in1=junk[:, :],
                                       op0=ALU.is_ge, op1=ALU.mult)
                dve.drain()
                V.scalar_tensor_tensor(out=a_buf[:, :], in0=tie[:, :], scalar=lo[:, :], in1=a_buf[:, :],
                                       op0=ALU.mult, op1=ALU.add, accum_out=kept[:, :])
                dve.drain()
                V.memset(tie[:, N:NP], 0.0)
                dve.drain()

            def verdict():
                V.tensor_scalar(bad[:, 0:1], kept[:, :], tgt[:, 1:2], 100.0, ALU.is_lt, ALU.mult)
                V.tensor_scalar(bad[:, 1:2], kept[:, :], tau[:, :], tgt[:, 0:1], ALU.subtract, ALU.is_ge)
                dve.drain()
                V.tensor_tensor(flag[:, 0:1], bad[:, 0:1], bad[:, 1:2], ALU.add)
                dve.drain()
                V.transpose(flag_t[:, :], flag[:, :])
                dve.drain()
                V.tensor_reduce(flag_i[:, :], flag_t[:, :], AX, ALU.max)
                dve.drain()
                worst = [V.value_load(flag_i[32 * q:32 * q + 1, 0:1]) for q in range(4)]
                return worst[0] + worst[1] + worst[2] + worst[3]

            def mask(step, k, par):
                g = chunk_base(step) + (8 if step == 0 else 10) * k
                dve.wait_ge(tr_done, g - (1 if step == 0 else 3))
                threshold(par)
                first = verdict()
                with dve.If(first > 0):
                    with dve.If(first > 99):
                        more_candidates(par, MORE_ROUNDS[0])
                        second = verdict()
                        with dve.If(second > 99):
                            more_candidates(par, MORE_ROUNDS[1])
                            third = verdict()
                            with dve.If(third > 99):
                                search_exactly(par)
                    drop_ties(par)
                V.reciprocal(inv_kept[par][:, :], kept[:, :]).then_inc(a_ready, 1)

            def inverse_sums(step, k):
                dve.wait_ge(s_ready, step * NT + k)
                if step == 0:
                    dve.wait_ge(adj_used, 4 * k + 6)
                    V.tensor_copy(inv_sum[:, 0:1], bank_s[:, D:D + 1])
                    V.scalar_tensor_tensor(out=junk[:, 0:P], in0=bank_s[:, D + 4:D + 4 + P], scalar=1.0,
                                           in1=ident[:, :], op0=ALU.mult, op1=ALU.mult,
                                           accum_out=inv_sum[:, 1:2])
                    dve.drain()
                    V.tensor_scalar(inv_sum[:, :], inv_sum[:, :], CLIP, None, ALU.max)
                    dve.drain()
                    V.reciprocal(inv_sum[:, :], inv_sum[:, :]).then_inc(inv_ready, 1)
                    dve.drain()
                    V.tensor_copy(inv_sums[:, bass.ds(2 * k, 2)], inv_sum[:, :])
                else:
                    V.tensor_copy(inv_sum[:, :], inv_sums[:, bass.ds(2 * k, 2)]).then_inc(inv_ready, 1)

            def row_max(step, k, par):
                dve.wait_ge(l_copied, NL * (step * NT + k) + NL)
                V.tensor_reduce(neg_max[par][:, :], e_buf[par][:, 0:N], AX, ALU.max,
                                negate=True).then_inc(max_ready, 1)

            for step in range(2):
                def iteration(k, par, begins, ends, ahead):
                    if ends and not begins:
                        inverse_sums(step, k - 1)
                    if begins:
                        last = HALVINGS[step] - 1
                        first = COARSE[step] if ends else 0
                        dve.wait_ge(coarse_ready, step * NT + k + 1)
                        targets(par)
                        search(par, range(first, first + ROW_MAX_AT), last)
                        if ends:
                            inverse_sums(step, k - 1)
                        if ahead:
                            row_max(step, k + 1, 1 - par)
                        search(par, range(first + ROW_MAX_AT, last + 1), last)
                        mask(step, k, par)
                    if ends and step == 1:
                        dve.wait_ge(tr_used, chunk_base(1) + 10 * (k - 1) + 12)
                        y = xs[:, bass.ds((k - 1) * W, D)]
                        V.tensor_tensor(y, bank_m[:, 0:D], y, ALU.add).then_inc(y_ready, 1)

                row_max(step, 0, 0)
                steps(dve, iteration)

            dve.drain()
            with dve.Fori(0, PAIRS) as pr:
                pair_stats(lambda k: xs[:, bass.ds(k * W, D)], pr)
            norms(2)
            dve.wait_ge(x_in, 32)
            dve.wait_ge(late_in, 64)
            for c in range(2):
                w_sa = wh_sb[:, c * WH:c * WH + D]
                for i, (a, w) in enumerate(((a_left, work), (a_right, work2))):
                    dve.drain()
                    V.scalar_tensor_tensor(out=w, in0=w_sa, scalar=-1.0, in1=a, op0=ALU.mult, op1=ALU.mult,
                                           accum_out=n_w[:, 2 * c + i:2 * c + i + 1])
            dve.drain()
            for c in range(2):
                V.tensor_scalar(w_left[:, c * P:(c + 1) * P], ones[:, :], n_w[:, 2 * c:2 * c + 1], None, ALU.mult)
                V.tensor_copy(wh_sb[:, c * WH + D + 2:c * WH + D + 3], n_w[:, 2 * c + 1:2 * c + 2])
            dve.drain().then_inc(w_left_ready, 1)
            with dve.Fori(0, PAIRS) as pr:
                both = [(2 * pr + u, (work, work2)[u]) for u in range(2)]
                for k, w in both:
                    V.tensor_scalar(w, xs[:, bass.ds(k * W, D)], rstd[:, bass.ds(k, 1)],
                                    shift[:, bass.ds(k, 1)], ALU.mult, ALU.add)
                dve.drain()
                for k, w in both:
                    V.tensor_tensor(w, w, gamma, ALU.mult)
                dve.drain()
                for k, w in both:
                    V.tensor_tensor(w, w, beta, ALU.add)
                dve.drain()
                for k, w in both:
                    V.tensor_tensor(x1[:, bass.ds(k * D, D)], x1[:, bass.ds(k * D, D)], w, ALU.add)
                dve.drain()
                pair_stats(lambda k: x1[:, bass.ds(k * D, D)], pr)
            norms(3)
            copy_rows(chunk_base(2), NT)

            n_sr = hb[:, :].rearrange("p (k t) -> p k t", t=3)[:, :, 2]

            def scores(k):
                grid = a_buf[:, :].rearrange("p (j c) -> p j c", c=P)
                V.tensor_tensor(grid, slb[:, bass.ds(k * P, P)].unsqueeze(1).to_broadcast([P, NT, P]),
                                n_sr.unsqueeze(2).to_broadcast([P, NT, P]), ALU.add)
                dve.drain()
                V.scalar_tensor_tensor(out=a_buf[:, :], in0=a_buf[:, :], scalar=0.01, in1=a_buf[:, :],
                                       op0=ALU.mult, op1=ALU.min).then_inc(score_ready, 1)

            def masked(k, par):
                dve.wait_ge(score_exp, k + 1)
                dve.wait_ge(full_in[par], 32 * (k // 2 + 1))
                dve.wait_ge(att_done, k + 1)
                V.scalar_tensor_tensor(out=kq[par][:, :], in0=e_buf[par][:, :], scalar=0.0, in1=a_buf[:, :],
                                       op0=ALU.not_equal, op1=ALU.mult).then_inc(et_ready, 1)

            def combine(k, par):
                att, gcn = bank_l[par], bank_l[2]
                dve.wait_ge(att_done, k + 3)
                dve.wait_ge(tr_used, chunk_base(2) + NT + k + 3)
                V.tensor_tensor(gate[:, 0:2], gcn[:, D:W], hb[:, bass.ds(3 * k, 2)], ALU.add)
                V.tensor_scalar(den[:, :], att[:, D:D + 1], 1e-5, None, ALU.add)
                dve.drain()
                V.tensor_tensor(gate[:, 0:2], gate[:, 0:2], gb_sb[:, :], ALU.add)
                V.tensor_tensor(work, gcn[:, 0:D], b_gcn, ALU.add)
                V.reciprocal(den[:, :], den[:, :])
                dve.drain()
                V.tensor_scalar(gate[:, 0:2], gate[:, 0:2], SIG_MIN, None, ALU.max).then_inc(gate_arg, 1)
                dve.wait_ge(gate_exp, k + 1)
                V.tensor_scalar(gate[:, 2:4], gate[:, 2:4], 1.0, None, ALU.add)
                dve.drain()
                V.reciprocal(gate[:, 2:4], gate[:, 2:4])
                dve.drain()
                V.tensor_tensor(den[:, :], den[:, :], gate[:, 2:3], ALU.mult)
                V.tensor_scalar(work, work, gate[:, 3:4], None, ALU.mult)
                dve.drain()
                V.scalar_tensor_tensor(out=work2, in0=att[:, 0:D], scalar=den[:, :], in1=work, op0=ALU.mult,
                                       op1=ALU.add)
                dve.drain()
                V.tensor_scalar(work2, work2, SIG_MIN, None, ALU.max).then_inc(comb_ready, 1)
                dve.wait_ge(comb_exp, k + 1)
                V.tensor_scalar(work2, work2, 1.0, None, ALU.add)
                dve.drain()
                V.reciprocal(work2, work2)
                dve.drain()
                dve.wait_ge(out_sent[par], 16 + 16 * (k // 2))
                V.tensor_tensor(out_st[par], work2, x1[:, bass.ds(k * D, D)], ALU.add).then_inc(out_ready, 1)

            def layer(k, par, begins, ends, ahead):
                if begins:
                    masked(k, par)
                dve.drain()
                if ahead:
                    scores(k + 1)
                if ends:
                    combine(k - 1, 1 - par)

            dve.wait_ge(sl_ready, 2)
            scores(0)
            steps(dve, layer)


INPUTS = ("x", "adj_t", "adj_n", "w1t", "w2", "w3", "u_all", "wh", "wg", "rows", "gate_bias")


def kernel(**inputs):
    import concourse.bacc as bacc
    from concourse.bass_utils import run_bass_kernel_spmd

    a = {k: np.asarray(v) for k, v in inputs.items()}
    f32 = np.float32

    x = np.zeros((NP, D), f32)
    x[:N] = a["x"]
    adj = np.zeros((NP, NP), f32)
    adj[:N, :N] = a["adj"]
    blocks = adj.reshape(NT, P, NT, P)

    def halves(b):
        return np.ascontiguousarray(b.reshape(NT, P, 2, HALF * P).transpose(0, 2, 1, 3)).reshape(
            2 * NT, P, HALF * P)

    def by_feature(w):
        return np.ascontiguousarray(w.reshape(2, P, -1).transpose(1, 0, 2)).reshape(P, -1)

    u = [a["L0_gnn_U1"][0], a["L0_gnn_U2"][0], a["L0_gnn_U1"][1], a["L0_gnn_U2"][1],
         a["L0_gnn_U3"][0], a["L0_gnn_U3"][1]]
    wa, wb = a["L1_gnn_Wa"][0], a["L1_gnn_Wb"][0]
    rows = np.concatenate([a["L0_gnn_gamma"], a["L0_gnn_beta"], a["L1_gnn_a_sa"][0], a["L1_gnn_b_gcnb"]])
    gate_bias = np.concatenate([a["L1_gnn_ba"], a["L1_gnn_bb"]])
    arrays = {
        "x": np.ascontiguousarray(x.reshape(NT, P, D).transpose(1, 0, 2)).reshape(P, NT * D),
        "adj_t": halves(blocks.transpose(0, 3, 2, 1)),
        "adj_n": halves(blocks.transpose(2, 1, 0, 3)),
        "w1t": np.ascontiguousarray(a["L0_gnn_W1"].T),
        "w2": a["L0_gnn_W2"],
        "w3": a["L0_gnn_W3"],
        "u_all": np.concatenate([by_feature(w) for w in u], axis=1),
        "wh": by_feature(np.concatenate([a["L1_gnn_W_sa"], wa[D:, None], wb[D:, None],
                                             np.zeros((D, WH - D - 2), f32)], axis=1)),
        "wg": by_feature(np.concatenate([a["L1_gnn_W_gcnb"], wa[:D, None], wb[:D, None]], axis=1)),
        "rows": np.ascontiguousarray(np.broadcast_to(rows, (P, rows.size))),
        "gate_bias": np.ascontiguousarray(np.broadcast_to(gate_bias, (P, 2))),
    }
    nc = bacc.Bacc("TRN2", target_bir_lowering=False, num_devices=1)
    args, fed = [], {}
    for name in INPUTS:
        fed[f"in_{name}"] = np.ascontiguousarray(arrays[name])
        args.append(nc.dram_tensor(f"in_{name}", arrays[name].shape, F32, kind="ExternalInput").ap())
    out = nc.dram_tensor("out", (N, D), F32, kind="ExternalOutput").ap()
    build(nc, *args, out)
    r = run_bass_kernel_spmd(nc, [fed], core_ids=[0])
    return r.results[0]["out"]
```

```python
from contextlib import ExitStack
from itertools import zip_longest

import numpy as np
import concourse.bass as bass
from concourse import mybir

F32 = mybir.dt.float32
U8 = mybir.dt.uint8
I8 = mybir.dt.int8
I32 = mybir.dt.int32
ALU = mybir.AluOpType
ACT = mybir.ActivationFunctionType
AX = mybir.AxisListType.X

P = 128
N = 3327
NT = -(-N // P)
NP = NT * P
D = 256
DA = 64
W = D + 2
WH = D + 4
HALF = NT // 2
LC = 512
NL = -(-N // LC)
AC = -(-NT // 4)
PAIRS = NT // 2
P_NUC = 0.9
LN_EPS = 1e-5
CLIP = 1e-12
SIG_MIN = -87.0

FLOOR = (1.0 - P_NUC) * 0.999 / N
SPAN = 1.01 / FLOOR
COARSE = (3, 5)
HALVINGS = (8, 11)
MORE_ROUNDS = (1, 3)
EXACT_STEPS = 42
EXACT_ROUNDS = 4
FILL = ((3,) * 7, (3,) * 7 + (6,))
ROW_MAX_AT = (2, 2)
SLACK = 4e-6


def chunk_base(step):
    return (NT, NT + 8 * NT, NT + 18 * NT)[step]


def build(nc, x, adj_t, w1t, w2, w3, u_all, wh, wg, rows, gate_bias, out):
    V = nc.vector
    with ExitStack() as ctx:
        def sb(name, shape, dt=F32):
            return ctx.enter_context(nc.sbuf_tensor(name, shape, dt))

        def ps(name, shape):
            return ctx.enter_context(nc.psum_tensor(name, shape, F32))

        def sem(name):
            return ctx.enter_context(nc.semaphore(name))

        xs = sb("xs", [P, NT * W])
        fb = sb("fb", [P, NT * 2 * D])
        xa = sb("xa", [P, NT * W])
        kq = [sb(f"kq{s}", [P, NP]) for s in range(2)]
        e_buf = [sb(f"e{i}", [P, NP]) for i in range(2)]
        a_buf = sb("a_buf", [P, NP])
        ring = sb("ring", [P, 2, HALF * P])
        tr = [sb(f"tr{i}", [P, 4 * P]) for i in range(2)]
        junk = sb("junk", [P, NP], U8)
        junk_act = sb("junk_act", [P, NP], I8)
        stage = sb("stage", [P, 6 * D])
        ident = sb("ident", [P, P])
        ones = sb("ones", [P, P])
        w_left = sb("w_left", [P, 2 * P])
        wqk = sb("wqk", [P, 2 * P])
        w1t_sb = sb("w1t_sb", [DA, D])
        w2_sb = sb("w2_sb", [DA, DA])
        q_st = [sb(f"q_st{i}", [P, P]) for i in range(2)]
        neg_max = [sb(f"neg_max{i}", [P, 1]) for i in range(2)]
        z = [sb(f"z{i}", [P, 1]) for i in range(2)]
        inv_kept = [sb(f"inv_kept{i}", [P, 1]) for i in range(2)]
        inv_sum = sb("inv_sum", [P, 2])
        inv_sums = sb("inv_sums", [P, 2 * NT])
        col_sums = sb("col_sums", [P, NT])
        col_part = sb("col_part", [P, NT])
        tgts = [sb(f"tgt{i}", [P, 2]) for i in range(2)]
        c_mid = [sb(f"c_mid{i}", [P, 1]) for i in range(2)]
        c_off = sb("c_off", [P, 1])
        c_tgt = sb("c_tgt", [P, 1])
        c_relu = sb("c_relu", [P, 1])
        c_sign = sb("c_sign", [P, 1])
        c_sum = sb("c_sum", [P, 1])
        c_step = sb("c_step", [P, 1])
        lo = sb("lo", [P, 1])
        hi = sb("hi", [P, 1])
        mids = [sb(f"mid{i}", [P, 1]) for i in range(2)]
        wid = sb("wid", [P, 1])
        inc = sb("inc", [P, 1])
        mass = sb("mass", [P, 1])
        next_mass = sb("next_mass", [P, 1])
        above = sb("above", [P, 1])
        top8 = sb("top8", [P, 8])
        cum8 = sb("cum8", [P, 8])
        tau = sb("tau", [P, 1])
        kept = sb("kept", [P, 1])
        bad = sb("bad", [P, 2])
        flag = sb("flag", [P, 32])
        flag_t = sb("flag_t", [P, 32])
        flag_i = sb("flag_i", [P, 1], I32)
        bst = [sb(f"bst{i}", [P, 6]) for i in range(2)]
        mv = sb("mv", [P, 4])
        mvs = sb("mvs", [P, 2 * NT])
        std = sb("std", [P, NT])
        rstd = sb("rstd", [P, NT])
        shift = sb("shift", [P, NT])
        hb = sb("hb", [P, 3 * NT])
        n_w = sb("n_w", [P, 4])
        gate = sb("gate", [P, 4])
        den = sb("den", [P, 1])
        gb_sb = sb("gb_sb", [P, 2])
        x1 = fb[:, 0:NT * D]
        slb = fb[:, NT * D:NT * D + NP]
        hh = xa
        u_sb = kq[0][:, 0:6 * 2 * D]
        flat_ring = ring[:, :, :].rearrange("p a b -> p (a b)")
        wh_sb = flat_ring[:, 0:2 * WH]
        wg_sb = flat_ring[:, 2 * WH:2 * WH + 2 * W]
        rows_sb = flat_ring[:, 2 * WH + 2 * W:2 * WH + 2 * W + 5 * D]
        gamma, beta, a_left, a_right, b_gcn = (rows_sb[:, i * D:(i + 1) * D] for i in range(5))
        ts_st = stage[:, 0:D]
        work = stage[:, 2 * D:3 * D]
        work2 = stage[:, 3 * D:4 * D]
        out_st = [stage[:, 4 * D:5 * D], stage[:, 5 * D:6 * D]]

        bank_l = [ps(f"bank_l{i}", [P, LC]) for i in range(3)]
        bank_t = [ps(f"bank_t{i}", [P, LC]) for i in range(2)]
        bank_xa = ps("bank_xa", [P, LC])
        bank_s = ps("bank_s", [P, LC])
        bank_m = ps("bank_m", [P, LC])
        chunk_bank = [*bank_t, *bank_l, *bank_t, *bank_l[:2], bank_t[1]]

        x_in = sem("x_in")
        w_in = sem("w_in")
        wqk_in = sem("wqk_in")
        u_in = sem("u_in")
        late_in = sem("late_in")
        const_ready = sem("const_ready")
        stats_ready = sem("stats_ready")
        std_ready = sem("std_ready")
        rstd_ready = sem("rstd_ready")
        h_ready = sem("h_ready")
        w12_done = sem("w12_done")
        w12_ready = sem("w12_ready")
        tr_done = sem("tr_done")
        tr_ready = sem("tr_ready")
        tr_used = sem("tr_used")
        kq_ready = sem("kq_ready")
        q_in = [sem(f"q_in{i}") for i in range(2)]
        l_done = sem("l_done")
        l_copied = sem("l_copied")
        max_ready = sem("max_ready")
        coarse_ready = sem("coarse_ready")
        a_ready = sem("a_ready")
        xa_ready = sem("xa_ready")
        adj_in = [sem(f"adj_in{i}") for i in range(2)]
        adj_used = sem("adj_used")
        adj_added = sem("adj_added")
        xb_ready = sem("xb_ready")
        inv_ready = sem("inv_ready")
        s_ready = sem("s_ready")
        y_ready = sem("y_ready")
        staged = sem("staged")
        w_left_ready = sem("w_left_ready")
        sl_ready = sem("sl_ready")
        hh_ready = sem("hh_ready")
        full_in = [sem(f"full_in{i}") for i in range(2)]
        score_ready = sem("score_ready")
        score_exp = sem("score_exp")
        et_ready = sem("et_ready")
        ts_done = sem("ts_done")
        ts_ready = sem("ts_ready")
        att_done = sem("att_done")
        gate_arg = sem("gate_arg")
        gate_exp = sem("gate_exp")
        comb_ready = sem("comb_ready")
        comb_exp = sem("comb_exp")
        out_ready = sem("out_ready")
        out_sent = [sem(f"out_sent{i}") for i in range(2)]

        block = ctx.enter_context(nc.Block())

        def steps(eng, iteration):
            iteration(0, 0, True, False, True)
            with eng.Fori(0, PAIRS - 1) as pr:
                iteration(2 * pr + 1, 1, True, True, True)
                iteration(2 * pr + 2, 0, True, True, True)
            iteration(NT - 1, 1, True, True, False)
            iteration(NT, 0, False, True, False)

        @block.sync
        def _(sp):
            for u in range(2):
                sp.sem_inc(out_sent[u], 16)
            for from_one in (kq_ready, xa_ready, a_ready, y_ready, hh_ready, sl_ready, ts_ready):
                sp.sem_inc(from_one, 1)
            sp.dma_start(x1, x).then_inc(x_in, 16)
            sp.dma_start(w1t_sb[:, :], w1t).then_inc(w_in, 16)
            sp.dma_start(w2_sb[:, :], w2).then_inc(w_in, 16)
            for c in range(2):
                sp.dma_start(wqk[:, c * P:c * P + DA], w3[c * P:(c + 1) * P, :]).then_inc(wqk_in, 16)

            def load_q(step, k, par):
                sp.dma_start(q_st[par][0:DA, :], kq[step][DA:P, bass.ds(k * P, P)]).then_inc(q_in[par], 16)

            def load_adj(step, k):
                for half in range(2):
                    piece = 2 * (step * NT + k) + half
                    sp.wait_ge(adj_used, piece + 1)
                    if step == 0:
                        sp.wait_ge(adj_added, piece + 1)
                    sp.dma_start(ring[:, half, :], adj_t[bass.ds(2 * k + half, 1), :, :].rearrange(
                        "a p n -> (a p) n")).then_inc(adj_in[half], 16)

            for step in range(2):
                sp.wait_ge(kq_ready, 1 + (step + 1) * NT)
                load_q(step, 0, 0)
                load_q(step, 1, 1)
                if step == 1:
                    sp.wait_ge(adj_added, 2 * NT + 2)
                    sp.wait_ge(l_done, NL * NT)
                    sp.dma_start(u_sb, u_all).then_inc(u_in, 16)
                with sp.Fori(0, PAIRS - 1) as pr:
                    for u in range(2):
                        sp.wait_ge(l_done, NL * (step * NT + 2 * pr + u + 1))
                        load_q(step, 2 * pr + u + 2, u)
                        load_adj(step, 2 * pr + u)
                for u in range(2):
                    load_adj(step, NT - 2 + u)
            sp.wait_ge(adj_used, 4 * NT + 2)
            sp.wait_ge(y_ready, 1 + NT)
            sp.dma_start(wh_sb, wh).then_inc(late_in, 16)
            sp.dma_start(wg_sb, wg).then_inc(late_in, 16)
            sp.dma_start(rows_sb, rows).then_inc(late_in, 16)
            sp.dma_start(gb_sb[:, :], gate_bias).then_inc(late_in, 16)
            sp.dma_start(x1, x).then_inc(x_in, 16)

            def load_full(k, par):
                for half in range(2):
                    sp.dma_start(e_buf[par][:, half * HALF * P:(half + 1) * HALF * P],
                                 adj_t[bass.ds(2 * k + half, 1), :, :].rearrange("a p n -> (a p) n")
                                 ).then_inc(full_in[par], 16)

            def store(k, par):
                sp.wait_ge(out_ready, k + 1)
                sp.dma_start(out[bass.ds(k * P, P), :], out_st[par]).then_inc(out_sent[par], 16)

            sp.wait_ge(a_ready, 1 + 2 * NT)
            sp.wait_ge(tr_ready, chunk_base(2) + 2)
            load_full(0, 0)
            load_full(1, 1)
            with sp.Fori(0, PAIRS - 1) as pr:
                for u in range(2):
                    sp.wait_ge(et_ready, 2 * pr + u + 1)
                    sp.wait_ge(ts_done, 2 * pr + u + 1)
                    load_full(2 * pr + u + 2, u)
                    store(2 * pr + u, u)
            store(NT - 2, 0)
            sp.wait_ge(out_ready, NT)
            sp.dma_start(out[(NT - 1) * P:N, :], out_st[1][0:N - (NT - 1) * P, :]).then_inc(out_sent[1], 16)
            for u in range(2):
                sp.wait_ge(out_sent[u], 16 + 16 * PAIRS)

        @block.gpsimd
        def _(pool):
            nc.gpsimd.memset(ident[:, :], 0.0)
            nc.gpsimd.memset(ones[:, :], 1.0)
            nc.gpsimd.memset(flag[:, :], 0.0)
            nc.gpsimd.memset(col_sums[:, :], 1.0)
            for q in q_st:
                nc.gpsimd.memset(q[:, :], 0.0)
            for e in e_buf:
                nc.gpsimd.memset(e[:, N:NP], 0.0)
            for rows_with_ones in (xs, xa):
                cols = rows_with_ones[:, :].rearrange("p (k w) -> p k w", w=W)
                nc.gpsimd.memset(cols[:, :, D:W], 1.0)
            pool.drain()
            nc.gpsimd.affine_select(out=ident[:, :], in_=ident[:, :], compare_op=ALU.not_equal, fill=1.0,
                                    base=0, pattern=[[-1, P]], channel_multiplier=1)
            pool.drain().then_inc(const_ready, 1)
            pool.wait_ge(xb_ready, 1)
            pool.wait_ge(xa_ready, 1 + NT)
            with pool.Fori(0, NT) as k:
                pool.wait_ge(tr_done, chunk_base(1) + 10 * k)
                nc.gpsimd.tensor_copy(stage[:, 0:2 * D], fb[:, bass.ds(k * 2 * D, 2 * D)])
                nc.gpsimd.tensor_copy(stage[:, 4 * D:5 * D], xa[:, bass.ds(k * W, D)])
                pool.drain().then_inc(staged, 1)

        @block.tensor
        def _(pe):
            mm = nc.tensor.matmul
            pe.sem_inc(adj_used, 2)
            pe.sem_inc(tr_used, 2)
            pe.sem_inc(att_done, 2)
            pe.wait_ge(const_ready, 1)
            pe.wait_ge(w_in, 32)
            for c in range(2):
                last = mm(bank_m[:, c * DA:(c + 1) * DA], w1t_sb[:, c * P:(c + 1) * P], w2_sb[:, :],
                          start=True, stop=True)
            last.then_inc(w12_done, 1)
            pe.wait_ge(w12_ready, 1)
            pe.wait_ge(wqk_in, 32)

            def transpose_blocks(bank, blocks):
                for b, source in enumerate(blocks):
                    last = nc.tensor.transpose(bank[:, b * P:(b + 1) * P], source, ident[:, :])
                last.then_inc(tr_done, 1)

            def transpose_chunk(g, par, blocks):
                pe.wait_ge(tr_ready, g + 1)
                transpose_blocks(bank_t[par], blocks)

            def use_chunk(g, par, products):
                pe.wait_ge(tr_ready, g + 3)
                for o, b, other, start, stop in products:
                    last = mm(o, tr[par][:, b * P:(b + 1) * P], other, start=start, stop=stop)
                last.then_inc(tr_used, 1)

            def two_blocks(rows):
                return rows[:, 0:P], rows[:, P:2 * P]

            def project_kq(g, par, m):
                pe.wait_ge(tr_ready, g + 3)
                pe.wait_ge(kq_ready, 1 + m)
                for c in range(2):
                    last = mm(bank_m[:, 0:P], wqk[:, c * P:(c + 1) * P], tr[par][:, c * P:(c + 1) * P],
                              start=(c == 0), stop=(c == 1))
                last.then_inc(tr_used, 1)

            def first_kq(k, par, begins, ends, ahead):
                if begins:
                    pe.wait_ge(h_ready, k + 1)
                    transpose_chunk(k, par, two_blocks(stage[:, (4 + par) * D:(5 + par) * D]))
                if ends:
                    project_kq(k - 1, 1 - par, k - 1)

            steps(pe, first_kq)

            def logits(step, k, par, chunks):
                n = step * NT + k
                pe.wait_ge(q_in[par], 16 * (step * PAIRS + k // 2 + 1))
                for c in chunks:
                    width = min(LC, N - c * LC)
                    pe.wait_ge(l_copied, NL * n + c - 2 if c >= 3 else NL * n)
                    mm(bank_l[c % 3][:, 0:width], q_st[par][:, :], kq[step][:, c * LC:c * LC + width],
                       start=True, stop=True).then_inc(l_done, 1)

            def s_product(step, k):
                pe.wait_ge(s_ready, step * NT + k)
                src, row, width = (xs, W, D + 1) if step == 0 else (fb, 2 * D, 2 * D)
                mm(bank_s[:, 0:width], ident[:, :], src[:, bass.ds(k * row, width)], start=True, stop=False)
                yield
                for half in range(2):
                    pe.wait_ge(adj_in[half], 16 * (step * NT + k + 1))
                    for b in range(HALF):
                        j = half * HALF + b
                        last = mm(bank_s[:, 0:width], ring[:, half, b * P:(b + 1) * P],
                                  src[:, j * row:j * row + width], start=False, stop=(j == NT - 1))
                        if b == HALF - 1:
                            last.then_inc(adj_used, 1)
                        yield

            def some(work, n):
                for _ in range(n):
                    next(work, None)

            def a_product(step, k, between, n_between, logits_out, first_logits):
                n = step * NT + k
                g = chunk_base(step) + (8 if step == 0 else 10) * k
                src = xs if step == 0 else xa
                pe.wait_ge(a_ready, 1 + n + 1)

                def product(c):
                    if c == 0:
                        pe.wait_ge(xa_ready, 1 + n)
                    use_chunk(g + c, c % 2, [(bank_xa[:, 0:D], j % 4, src[:, j * W:j * W + D],
                                              j == 0, j == NT - 1) for j in range(4 * c, min(4 * c + 4, NT))])

                def four_blocks(c):
                    return [stage[:, (4 * c + b) * P:(4 * c + b + 1) * P] for b in range(4)]

                def transpose_a(c):
                    transpose_blocks(chunk_bank[c], [a_buf[:, j * P:(j + 1) * P]
                                                     for j in range(4 * c, min(4 * c + 4, NT))])

                pe.wait_ge(tr_ready, g + 2)
                transpose_a(0)
                transpose_a(1)
                pe.wait_ge(l_copied, logits_out)
                for c in range(2, 5):
                    transpose_a(c)
                for c in range(AC):
                    if c < 2:
                        pe.wait_ge(tr_ready, g + c + 3)
                        transpose_a(5 + c)
                    product(c)
                    if step == 1 and c == 4:
                        pe.wait_ge(staged, k + 1)
                        pe.wait_ge(s_ready, n + 1)
                        pe.wait_ge(tr_ready, g + 6)
                        transpose_blocks(chunk_bank[7], four_blocks(0))
                        transpose_blocks(chunk_bank[8], four_blocks(1))
                    some(between, n_between[c])
                if step == 0:
                    first_logits()
                    pe.wait_ge(xa_ready, 1 + n + 1)
                    transpose_chunk(g + 7, 1, two_blocks(stage[:, 5 * D:6 * D]))
                    project_kq(g + 7, 1, NT + k)
                    return

                def z_product(c):
                    use_chunk(g + 7 + c, (7 + c) % 2,
                              [(bank_m[:, 0:D], b, u_sb[:, (4 * c + b) * D:(4 * c + b + 1) * D],
                                c == 0 and b == 0, c == 2 and b == 3) for b in range(4)])

                pe.wait_ge(u_in, 16)
                pe.wait_ge(kq_ready, 1 + 2 * NT)
                pe.wait_ge(y_ready, 1 + k)
                z_product(0)
                some(between, n_between[AC])
                pe.wait_ge(xa_ready, 1 + n + 1)
                transpose_chunk(g + 9, 1, four_blocks(2))
                z_product(1)
                first_logits()
                z_product(2)

            for step in range(2):
                def iteration(k, par, begins, ends, ahead, two_ahead):
                    between = s_product(step, k) if begins else iter(())

                    def first_logits():
                        if two_ahead:
                            logits(step, k + 2, par, range(3))

                    if ahead:
                        logits(step, k + 1, 1 - par, range(3, NL))
                    if ends:
                        a_product(step, k - 1, between, FILL[step],
                                  NL * (step * NT + (k + 2 if ahead else NT)), first_logits)
                    else:
                        first_logits()
                    for _ in between:
                        pass

                logits(step, 0, 0, range(NL))
                logits(step, 1, 1, range(3))
                if step == 1:
                    pe.wait_ge(xb_ready, 1)
                iteration(0, 0, True, False, True, True)
                with pe.Fori(0, PAIRS - 2) as pr:
                    iteration(2 * pr + 1, 1, True, True, True, True)
                    iteration(2 * pr + 2, 0, True, True, True, True)
                iteration(NT - 3, 1, True, True, True, True)
                iteration(NT - 2, 0, True, True, True, False)
                iteration(NT - 1, 1, True, True, False, False)
                iteration(NT, 0, False, True, False, False)

            pe.wait_ge(late_in, 64)
            pe.wait_ge(w_left_ready, 1)

            def h_product(k, par, begins, ends, ahead):
                if begins:
                    pe.wait_ge(h_ready, NT + k + 1)
                    transpose_chunk(chunk_base(2) + k, par, two_blocks(stage[:, (4 + par) * D:(5 + par) * D]))
                if ends:
                    t = tr[1 - par]
                    pe.wait_ge(tr_ready, chunk_base(2) + k - 1 + 3)
                    pe.wait_ge(hh_ready, 1 + k - 1)
                    for c in range(2):
                        mm(bank_s[:, 0:WH], t[:, c * P:(c + 1) * P], wh_sb[:, c * WH:(c + 1) * WH],
                           start=(c == 0), stop=(c == 1))
                    for c in range(2):
                        last = mm(bank_m[:, 0:P], w_left[:, c * P:(c + 1) * P], t[:, c * P:(c + 1) * P],
                                  start=(c == 0), stop=(c == 1))
                    last.then_inc(tr_used, 1)

            steps(pe, h_product)

            def layer(k, par):
                g = chunk_base(2) + NT + k
                pe.wait_ge(full_in[par], 32 * (k // 2 + 1))
                pe.wait_ge(ts_ready, 1 + k)
                for j in range(NT):
                    last = mm(bank_xa[:, 0:D], e_buf[par][:, j * P:(j + 1) * P], xs[:, j * W:j * W + D],
                              start=(j == 0), stop=(j == NT - 1))
                last.then_inc(ts_done, 1)
                pe.wait_ge(et_ready, k + 1)
                pe.wait_ge(comb_ready, k + 1)
                for j in range(NT):
                    last = mm(bank_l[par][:, 0:D + 1], kq[par][:, j * P:(j + 1) * P], hh[:, j * W:j * W + D + 1],
                              start=(j == 0), stop=(j == NT - 1))
                last.then_inc(att_done, 1)
                pe.wait_ge(ts_ready, 1 + k + 1)
                transpose_chunk(g, par, two_blocks(ts_st))
                pe.wait_ge(comb_ready, k + 2)
                use_chunk(g, par, [(bank_l[2][:, 0:W], c, wg_sb[:, c * W:(c + 1) * W], c == 0, c == 1)
                                   for c in range(2)])

            pe.wait_ge(hh_ready, 1 + NT)
            with pe.Fori(0, PAIRS) as pr:
                for u in range(2):
                    layer(2 * pr + u, u)

        @block.scalar
        def _(act):
            def copy(dst, src, scale=1.0):
                return nc.scalar.activation(dst, src, ACT.Copy, scale=scale)

            act.sem_inc(tr_ready, 2)

            def copy_chunk(g, par, width, bank=None):
                act.wait_ge(tr_done, g + 1)
                act.wait_ge(tr_used, g + 1)
                copy(tr[par][:, 0:width], (bank or bank_t[par])[:, 0:width]).then_inc(tr_ready, 1)

            def root(count):
                act.wait_ge(stats_ready, count)
                nc.scalar.activation(std[:, :], std[:, :], ACT.Sqrt).then_inc(std_ready, 1)
                act.wait_ge(rstd_ready, count)

            def norm_relu(dst, k):
                return nc.scalar.activation(dst, x1[:, bass.ds(k * D, D)], ACT.Relu,
                                            bias=shift[:, bass.ds(k, 1)], scale=rstd[:, bass.ds(k, 1)])

            act.wait_ge(w12_done, 1)
            for c in range(2):
                last = copy(wqk[:, c * P + DA:(c + 1) * P], bank_m[:, c * DA:(c + 1) * DA])
            last.then_inc(w12_ready, 1)
            root(1)

            def first_kq(k, par, begins, ends, ahead):
                if ahead:
                    act.wait_ge(tr_ready, k + 2)
                    norm_relu(stage[:, (5 - par) * D:(6 - par) * D], k + 1).then_inc(h_ready, 1)
                if ends:
                    act.wait_ge(tr_used, k + 2)
                    copy(kq[0][:, bass.ds((k - 1) * P, P)], bank_m[:, 0:P]).then_inc(kq_ready, 1)

            norm_relu(stage[:, 4 * D:5 * D], 0).then_inc(h_ready, 1)
            steps(act, first_kq)

            def chunk_of(step, k):
                return chunk_base(step) + (8 if step == 0 else 10) * k

            def copy_logits(step, k, par):
                n = step * NT + k
                for c in range(NL):
                    width = min(LC, N - c * LC)
                    act.wait_ge(l_done, NL * n + c + 1)
                    if c == 0:
                        act.wait_ge(a_ready, n)
                    copy(e_buf[par][:, c * LC:c * LC + width], bank_l[c % 3][:, 0:width]).then_inc(l_copied, 1)

            def exps(step, k, par):
                act.drain()
                act.wait_ge(max_ready, step * NT + k + 1)
                nc.scalar.activation(e_buf[par][:, 0:N], e_buf[par][:, 0:N], ACT.Exp, bias=neg_max[par][:, :],
                                     accum_out=z[par][:, :])
                act.drain()

            def coarse_start(par):
                copy(c_tgt[:, :], z[par][:, :], 4.0 * P_NUC)
                copy(c_mid[par][:, :], z[par][:, :], -2.0 * FLOOR * SPAN ** 0.5)

            def coarse_sums(par):
                act.drain()
                nc.scalar.activation(c_off[:, :], c_mid[par][:, :], ACT.Identity, scale=float(N), bias=c_tgt[:, :])
                act.drain()
                nc.scalar.activation(junk_act[:, 0:N], e_buf[par][:, 0:N], ACT.Relu, scale=2.0, bias=c_mid[par][:, :],
                                     accum_out=c_relu[:, :])

            def coarse_count(par):
                act.drain()
                nc.scalar.activation(junk_act[:, 0:N], e_buf[par][:, 0:N], ACT.Sign, scale=2.0, bias=c_mid[par][:, :],
                                     accum_out=c_sign[:, :])

            def coarse_move(par, level, last):
                act.drain()
                nc.scalar.activation(c_sum[:, :], c_sign[:, :], ACT.Identity, scale=c_mid[par][:, :],
                                     bias=c_off[:, :])
                act.drain()
                nc.scalar.activation(c_step[:, :], c_relu[:, :], ACT.Sign, scale=-2.0, bias=c_sum[:, :])
                act.drain()
                nc.scalar.activation(c_step[:, :], c_step[:, :], ACT.Exp,
                                     scale=-float(np.log(SPAN) * 0.5 ** (level + 2)))
                act.drain()
                moved = copy(c_mid[par][:, :], c_mid[par][:, :], c_step[:, :])
                if last:
                    moved.then_inc(coarse_ready, 1)

            def ahead_parts(step, k, par):
                parts = [lambda: (exps(step, k, par), coarse_start(par))]
                for level in range(COARSE[step]):
                    parts += [lambda: coarse_sums(par),
                              lambda level=level: (coarse_count(par),
                                                   coarse_move(par, level, level == COARSE[step] - 1))]
                return parts

            def out_of_s(step, k):
                act.wait_ge(inv_ready, step * NT + k + 1)
                act.wait_ge(adj_used, 2 * (step * NT + k) + 4)
                if step == 0:
                    copy(fb[:, bass.ds(k * 2 * D, D)], bank_s[:, 0:D], inv_sum[:, 0:1])
                    copy(fb[:, bass.ds(k * 2 * D + D, D)], bank_s[:, 0:D]).then_inc(s_ready, 1)
                else:
                    copy(stage[:, 2 * D:3 * D], bank_s[:, 0:D], inv_sum[:, 0:1])
                    copy(stage[:, 3 * D:4 * D], bank_s[:, D:2 * D], inv_sum[:, 1:2]).then_inc(s_ready, 1)

            def end_parts(step, k, par):
                g = chunk_of(step, k)

                def xa_out():
                    act.wait_ge(tr_used, g + AC + 2)
                    if step == 0:
                        copy(xa[:, bass.ds(k * W, D)], bank_xa[:, 0:D], inv_kept[par][:, :])
                    copy(stage[:, 5 * D:6 * D], bank_xa[:, 0:D], inv_kept[par][:, :]).then_inc(xa_ready, 1)

                def kq_out():
                    act.wait_ge(tr_used, g + 10)
                    copy(kq[1][:, bass.ds(k * P, P)], bank_m[:, 0:P]).then_inc(kq_ready, 1)

                parts = [lambda c=c: copy_chunk(g + c, c % 2, P * min(4, NT - 4 * c), chunk_bank[c])
                         for c in range(AC)]
                if step == 0:
                    return parts + [xa_out, lambda: copy_chunk(g + 7, 1, 2 * P), kq_out]
                last = [lambda c=c: copy_chunk(g + c, c % 2, 4 * P, chunk_bank[c]) for c in (7, 8, 9)]
                return parts + [last[0], xa_out, *last[1:]]

            for step in range(2):
                def iteration(k, par, begins, ends, ahead):
                    coarse = ahead_parts(step, k + 1, 1 - par) if ahead else []
                    ending = end_parts(step, k - 1, 1 - par) if ends else []
                    if ahead:
                        copy_logits(step, k + 1, 1 - par)
                    if ends:
                        out_of_s(step, k - 1)
                    for end_part, coarse_part in zip_longest(ending, coarse):
                        for part in (end_part, coarse_part):
                            if part:
                                part()

                copy_logits(step, 0, 0)
                exps(step, 0, 0)
                copy(c_mid[0][:, :], z[0][:, :], -2.0 * FLOOR * SPAN ** 0.5).then_inc(coarse_ready, 1)
                steps(act, iteration)

            root(2)
            root(3)

            def h_product(k, par, begins, ends, ahead):
                if ahead:
                    act.wait_ge(tr_ready, chunk_base(2) + k + 2)
                    norm_relu(stage[:, (5 - par) * D:(6 - par) * D], k + 1).then_inc(h_ready, 1)
                if ends:
                    act.wait_ge(tr_used, chunk_base(2) + k + 2)
                    copy(hh[:, bass.ds((k - 1) * W, D)], bank_s[:, 0:D])
                    copy(hb[:, bass.ds(3 * (k - 1), 3)], bank_s[:, D:D + 3])
                    copy(slb[:, bass.ds((k - 1) * P, P)], bank_m[:, 0:P]).then_inc(hh_ready, 1)

            norm_relu(stage[:, 4 * D:5 * D], 0).then_inc(h_ready, 1)
            steps(act, h_product)
            act.drain().then_inc(sl_ready, 1)

            def score_exps(k):
                act.wait_ge(score_ready, k + 1)
                nc.scalar.activation(a_buf[:, :], a_buf[:, :], ACT.Exp).then_inc(score_exp, 1)

            def layer(k, par, begins, ends, ahead):
                if ahead:
                    score_exps(k + 1)
                if ends:
                    copy_chunk(chunk_base(2) + NT + k - 1, 1 - par, 2 * P)
                    act.wait_ge(gate_arg, k)
                    nc.scalar.activation(gate[:, 2:4], gate[:, 0:2], ACT.Exp, scale=-1.0).then_inc(gate_exp, 1)
                    act.wait_ge(comb_ready, k + 2)
                    nc.scalar.activation(work2, work2, ACT.Exp, scale=-1.0).then_inc(comb_exp, 1)
                if begins:
                    act.wait_ge(ts_done, k + 1)
                    copy(ts_st, bank_xa[:, 0:D]).then_inc(ts_ready, 1)

            score_exps(0)
            steps(act, layer)

        @block.vector
        def _(dve):
            dve.sem_inc(comb_ready, 2)
            dve.sem_inc(adj_added, 2)
            dve.wait_ge(const_ready, 1)

            def pair_stats(src, pr):
                for u in range(2):
                    V.bn_stats(bst[u][:, :], src(2 * pr + u))
                dve.drain()
                for u in range(2):
                    V.bn_aggr(mv[:, 2 * u:2 * u + 2], bst[u][:, :])
                dve.drain()
                V.tensor_copy(mvs[:, bass.ds(4 * pr, 4)], mv[:, :])

            def copy_rows(first, h_first):
                with dve.Fori(0, PAIRS) as pr:
                    for u in range(2):
                        k = 2 * pr + u
                        dve.wait_ge(h_ready, h_first + k + 1)
                        V.tensor_copy(xs[:, bass.ds(k * W, D)], stage[:, (4 + u) * D:(5 + u) * D])
                        dve.wait_ge(tr_done, first + k + 1)
                        dve.wait_ge(tr_used, first + k + 1)
                        V.tensor_copy(tr[u][:, 0:2 * P], bank_t[u][:, 0:2 * P])
                        dve.drain().then_inc(tr_ready, 1)

            def norms(count):
                both = mvs[:, :].rearrange("p (k t) -> p k t", t=2)
                dve.drain()
                V.tensor_scalar(std[:, :], both[:, :, 1], LN_EPS, None, ALU.add).then_inc(stats_ready, 1)
                dve.wait_ge(std_ready, count)
                V.reciprocal(rstd[:, :], std[:, :])
                dve.drain()
                V.scalar_tensor_tensor(out=shift[:, :], in0=both[:, :, 0], scalar=-1.0, in1=rstd[:, :],
                                       op0=ALU.mult, op1=ALU.mult).then_inc(rstd_ready, 1)

            dve.wait_ge(x_in, 16)
            with dve.Fori(0, PAIRS) as pr:
                pair_stats(lambda k: x1[:, bass.ds(k * D, D)], pr)
            norms(1)
            copy_rows(0, 0)

            def mass_above(e, bound):
                V.scalar_tensor_tensor(out=junk[:, 0:N], in0=e[:, 0:N], scalar=bound, in1=e[:, 0:N],
                                       op0=ALU.is_ge, op1=ALU.mult, accum_out=mass[:, :])
                dve.drain()

            def targets(par):
                V.tensor_scalar(tgts[par][:, 0:1], z[par][:, :], P_NUC, None, ALU.mult)
                V.tensor_scalar(tgts[par][:, 1:2], z[par][:, :], P_NUC, 1.0 - SLACK, ALU.mult, ALU.mult)
                V.tensor_scalar(mids[par][:, :], c_mid[par][:, :], -0.5, None, ALU.mult)
                dve.drain()

            def start_search(par):
                targets(par)
                V.scalar_tensor_tensor(out=junk[:, 0:N], in0=e_buf[par][:, 0:N], scalar=mids[par][:, :],
                                       in1=e_buf[par][:, 0:N], op0=ALU.is_ge, op1=ALU.mult,
                                       accum_out=next_mass[:, :])

            def search(par, levels, last, started=False):
                mid, tgt = mids[par], tgts[par]
                for i in levels:
                    if started and i == levels[0]:
                        found = next_mass
                        dve.drain()
                    else:
                        found = mass
                        mass_above(e_buf[par], mid[:, :])
                    ratio = SPAN ** (0.5 ** (i + 1 if i == last else i + 2))
                    down = 1.0 if i == last else 1.0 / ratio
                    V.tensor_scalar(inc[:, :], found[:, :], tgt[:, 0:1], ratio - down, ALU.is_ge, ALU.mult)
                    dve.drain()
                    V.scalar_tensor_tensor(out=hi[:, :] if i == last else mid[:, :], in0=inc[:, :], scalar=down,
                                           in1=mid[:, :], op0=ALU.add, op1=ALU.mult)
                    dve.drain()

            def threshold(par):
                e, tgt = e_buf[par], tgts[par]
                V.scalar_tensor_tensor(out=a_buf[:, :], in0=e[:, :], scalar=hi[:, :], in1=e[:, :],
                                       op0=ALU.is_lt, op1=ALU.mult, accum_out=mass[:, :])
                dve.drain()
                V.max(top8[:, :], a_buf[:, :])
                V.tensor_scalar(above[:, :], mass[:, :], -1.0, z[par][:, :], ALU.mult, ALU.add)
                dve.drain()
                V.tensor_tensor(above[:, :], above[:, :], tgt[:, 1:2], ALU.min)
                dve.drain()
                V.tensor_tensor_scan(cum8[:, :], top8[:, :], top8[:, :], above[:, :], ALU.add, ALU.max)
                dve.drain()
                V.tensor_tensor(cum8[:, :], cum8[:, :], top8[:, :], ALU.subtract)
                dve.drain()
                V.tensor_scalar(cum8[:, :], cum8[:, :], tgt[:, 0:1], 4.0, ALU.is_ge, ALU.mult)
                dve.drain()
                V.tensor_tensor(cum8[:, :], cum8[:, :], top8[:, :], ALU.add)
                dve.drain()
                V.tensor_reduce(tau[:, :], cum8[:, :], AX, ALU.min)
                dve.drain()
                V.scalar_tensor_tensor(out=a_buf[:, :], in0=e[:, :], scalar=tau[:, :], in1=e[:, :],
                                       op0=ALU.is_ge, op1=ALU.mult, accum_out=kept[:, :])
                dve.drain()

            def more_candidates(par, rounds):
                tgt = tgts[par]
                with dve.Fori(0, rounds):
                    V.tensor_scalar(bad[:, 0:1], kept[:, :], tgt[:, 1:2], None, ALU.is_lt)
                    V.tensor_tensor(inc[:, :], tau[:, :], hi[:, :], ALU.subtract)
                    dve.drain()
                    V.scalar_tensor_tensor(out=hi[:, :], in0=inc[:, :], scalar=bad[:, 0:1], in1=hi[:, :],
                                           op0=ALU.mult, op1=ALU.add)
                    dve.drain()
                    threshold(par)

            def search_exactly(par):
                e, mid, tgt = e_buf[par], mids[par], tgts[par]
                V.tensor_scalar(lo[:, :], z[par][:, :], FLOOR, None, ALU.mult)
                V.memset(wid[:, :], 1.01)
                dve.drain()
                with dve.Fori(0, EXACT_STEPS):
                    V.tensor_scalar(wid[:, :], wid[:, :], 0.5, None, ALU.mult)
                    dve.drain()
                    V.tensor_tensor(mid[:, :], lo[:, :], wid[:, :], ALU.add)
                    dve.drain()
                    mass_above(e, mid[:, :])
                    V.scalar_tensor_tensor(out=inc[:, :], in0=mass[:, :], scalar=tgt[:, 0:1], in1=wid[:, :],
                                           op0=ALU.is_ge, op1=ALU.mult)
                    dve.drain()
                    V.tensor_tensor(lo[:, :], lo[:, :], inc[:, :], ALU.add)
                    dve.drain()
                V.scalar_tensor_tensor(out=hi[:, :], in0=lo[:, :], scalar=1.0 + 2.0 ** -22, in1=wid[:, :],
                                       op0=ALU.mult, op1=ALU.add)
                dve.drain()
                threshold(par)
                more_candidates(par, EXACT_ROUNDS)

            def drop_ties(par):
                tie, mid, tgt = e_buf[par], mids[par], tgts[par]
                dve.drain()
                V.tensor_scalar(junk[:, :], a_buf[:, :], tau[:, :], None, ALU.is_equal)
                V.reciprocal(inc[:, :], tau[:, :])
                V.tensor_tensor(mid[:, :], tgt[:, 0:1], kept[:, :], ALU.subtract)
                V.tensor_scalar(lo[:, :], tau[:, :], -1.0, None, ALU.mult)
                dve.drain()
                V.tensor_tensor_scan(tie[:, :], junk[:, :], junk[:, :], 0.0, ALU.add, ALU.max)
                V.scalar_tensor_tensor(out=mid[:, :], in0=mid[:, :], scalar=inc[:, :], in1=ones[:, 0:1],
                                       op0=ALU.mult, op1=ALU.add)
                dve.drain()
                V.tensor_tensor(mid[:, :], mid[:, :], tie[:, NP - 1:NP], ALU.add)
                dve.drain()
                V.scalar_tensor_tensor(out=tie[:, :], in0=tie[:, :], scalar=mid[:, :], in1=junk[:, :],
                                       op0=ALU.is_ge, op1=ALU.mult)
                dve.drain()
                V.scalar_tensor_tensor(out=a_buf[:, :], in0=tie[:, :], scalar=lo[:, :], in1=a_buf[:, :],
                                       op0=ALU.mult, op1=ALU.add, accum_out=kept[:, :])
                dve.drain()
                V.memset(tie[:, N:NP], 0.0)
                dve.drain()

            def verdict(par, ahead=False):
                tgt = tgts[par]
                V.tensor_scalar(bad[:, 0:1], kept[:, :], tgt[:, 1:2], 100.0, ALU.is_lt, ALU.mult)
                V.tensor_scalar(bad[:, 1:2], kept[:, :], tau[:, :], tgt[:, 0:1], ALU.subtract, ALU.is_ge)
                dve.drain()
                V.tensor_tensor(flag[:, 0:1], bad[:, 0:1], bad[:, 1:2], ALU.add)
                dve.drain()
                V.transpose(flag_t[:, :], flag[:, :])
                dve.drain()
                V.tensor_reduce(flag_i[:, :], flag_t[:, :], AX, ALU.max)
                dve.drain()
                if ahead:
                    start_search(1 - par)
                return last_verdict()

            def last_verdict():
                worst = [V.value_load(flag_i[32 * q:32 * q + 1, 0:1]) for q in range(4)]
                return worst[0] + worst[1] + worst[2] + worst[3]

            def mask(step, k, par, ahead):
                g = chunk_base(step) + (8 if step == 0 else 10) * k
                dve.wait_ge(tr_done, g - (1 if step == 0 else 3))
                threshold(par)
                if ahead:
                    dve.wait_ge(coarse_ready, step * NT + k + 2)
                first = verdict(par, ahead)
                with dve.If(first > 0):
                    with dve.If(first < 100):
                        drop_ties(par)
                    with dve.If(first > 99):
                        more_candidates(par, MORE_ROUNDS[0])
                        second = verdict(par)
                        with dve.If(second > 99):
                            more_candidates(par, MORE_ROUNDS[1])
                            third = verdict(par)
                            with dve.If(third > 99):
                                search_exactly(par)
                                verdict(par)
                        final = last_verdict()
                        with dve.If(final > 0):
                            drop_ties(par)
                V.reciprocal(inv_kept[par][:, :], kept[:, :]).then_inc(a_ready, 1)

            def inverse_sums(step, k):
                dve.wait_ge(s_ready, step * NT + k)
                if step == 0:
                    dve.wait_ge(adj_used, 2 * k + 4)
                    V.tensor_scalar(inv_sum[:, 0:1], bank_s[:, D:D + 1], CLIP, None, ALU.max)
                    dve.drain()
                    V.reciprocal(inv_sum[:, 0:1], inv_sum[:, 0:1]).then_inc(inv_ready, 1)
                    dve.drain()
                    V.tensor_copy(inv_sums[:, bass.ds(2 * k, 1)], inv_sum[:, 0:1])
                else:
                    V.tensor_copy(inv_sum[:, :], inv_sums[:, bass.ds(2 * k, 2)]).then_inc(inv_ready, 1)

            def add_columns(k):
                for half in range(2):
                    part = col_part[:, half * HALF:(half + 1) * HALF]
                    dve.wait_ge(adj_in[half], 16 * (k + 1))
                    V.tensor_reduce(part, ring[:, half, :].rearrange("p (b n) -> p b n", n=P), AX,
                                    ALU.add).then_inc(adj_added, 1)
                dve.drain()
                V.tensor_tensor(col_sums[:, :], col_sums[:, :], col_part[:, :], ALU.add)
                dve.drain()

            def scale_xb():
                inv_col = inv_sums[:, :].rearrange("p (k t) -> p k t", t=2)[:, :, 1]
                V.tensor_scalar(col_sums[:, :], col_sums[:, :], CLIP, None, ALU.max)
                dve.drain()
                V.reciprocal(inv_col, col_sums[:, :])
                dve.drain()
                dve.wait_ge(s_ready, NT)
                xb = fb[:, :].rearrange("p (k t) -> p k t", t=2 * D)[:, :, D:2 * D]
                V.tensor_tensor(xb, xb, inv_col.unsqueeze(2).to_broadcast([P, NT, D]),
                                ALU.mult).then_inc(xb_ready, 1)

            def row_max(step, k, par):
                dve.wait_ge(l_copied, NL * (step * NT + k) + NL)
                V.tensor_reduce(neg_max[par][:, :], e_buf[par][:, 0:N], AX, ALU.max,
                                negate=True).then_inc(max_ready, 1)

            for step in range(2):
                def iteration(k, par, begins, ends, ahead):
                    if ends and not begins:
                        inverse_sums(step, k - 1)
                    if begins:
                        last = HALVINGS[step] - 1
                        first = COARSE[step] if ends else 0
                        started = step == 0 and ends
                        if not started:
                            dve.wait_ge(coarse_ready, step * NT + k + 1)
                            targets(par)
                        search(par, range(first, first + ROW_MAX_AT[step]), last, started)
                        if ends:
                            inverse_sums(step, k - 1)
                        if ahead:
                            row_max(step, k + 1, 1 - par)
                        if step == 0:
                            add_columns(k)
                        search(par, range(first + ROW_MAX_AT[step], last + 1), last)
                        mask(step, k, par, ahead and step == 0)
                    if ends and step == 1:
                        dve.wait_ge(tr_used, chunk_base(1) + 10 * (k - 1) + 12)
                        y = xs[:, bass.ds((k - 1) * W, D)]
                        V.tensor_tensor(y, bank_m[:, 0:D], y, ALU.add).then_inc(y_ready, 1)

                if step == 1:
                    scale_xb()
                row_max(step, 0, 0)
                steps(dve, iteration)

            dve.drain()
            with dve.Fori(0, PAIRS) as pr:
                pair_stats(lambda k: xs[:, bass.ds(k * W, D)], pr)
            norms(2)
            dve.wait_ge(x_in, 32)
            dve.wait_ge(late_in, 64)
            for c in range(2):
                w_sa = wh_sb[:, c * WH:c * WH + D]
                for i, (a, w) in enumerate(((a_left, work), (a_right, work2))):
                    dve.drain()
                    V.scalar_tensor_tensor(out=w, in0=w_sa, scalar=-1.0, in1=a, op0=ALU.mult, op1=ALU.mult,
                                           accum_out=n_w[:, 2 * c + i:2 * c + i + 1])
            dve.drain()
            for c in range(2):
                V.tensor_scalar(w_left[:, c * P:(c + 1) * P], ones[:, :], n_w[:, 2 * c:2 * c + 1], None, ALU.mult)
                V.tensor_copy(wh_sb[:, c * WH + D + 2:c * WH + D + 3], n_w[:, 2 * c + 1:2 * c + 2])
            dve.drain().then_inc(w_left_ready, 1)
            with dve.Fori(0, PAIRS) as pr:
                both = [(2 * pr + u, (work, work2)[u]) for u in range(2)]
                for k, w in both:
                    V.tensor_scalar(w, xs[:, bass.ds(k * W, D)], rstd[:, bass.ds(k, 1)],
                                    shift[:, bass.ds(k, 1)], ALU.mult, ALU.add)
                dve.drain()
                for k, w in both:
                    V.tensor_tensor(w, w, gamma, ALU.mult)
                dve.drain()
                for k, w in both:
                    V.tensor_tensor(w, w, beta, ALU.add)
                dve.drain()
                for k, w in both:
                    V.tensor_tensor(x1[:, bass.ds(k * D, D)], x1[:, bass.ds(k * D, D)], w, ALU.add)
                dve.drain()
                pair_stats(lambda k: x1[:, bass.ds(k * D, D)], pr)
            norms(3)
            copy_rows(chunk_base(2), NT)

            n_sr = hb[:, :].rearrange("p (k t) -> p k t", t=3)[:, :, 2]

            def scores(k):
                grid = a_buf[:, :].rearrange("p (j c) -> p j c", c=P)
                V.tensor_tensor(grid, slb[:, bass.ds(k * P, P)].unsqueeze(1).to_broadcast([P, NT, P]),
                                n_sr.unsqueeze(2).to_broadcast([P, NT, P]), ALU.add)
                dve.drain()
                V.scalar_tensor_tensor(out=a_buf[:, :], in0=a_buf[:, :], scalar=0.01, in1=a_buf[:, :],
                                       op0=ALU.mult, op1=ALU.min).then_inc(score_ready, 1)

            def masked(k, par):
                dve.wait_ge(score_exp, k + 1)
                dve.wait_ge(full_in[par], 32 * (k // 2 + 1))
                dve.wait_ge(att_done, k + 1)
                V.scalar_tensor_tensor(out=kq[par][:, :], in0=e_buf[par][:, :], scalar=0.0, in1=a_buf[:, :],
                                       op0=ALU.not_equal, op1=ALU.mult).then_inc(et_ready, 1)

            def combine(k, par):
                att, gcn = bank_l[par], bank_l[2]
                dve.wait_ge(att_done, k + 3)
                dve.wait_ge(tr_used, chunk_base(2) + NT + k + 3)
                V.tensor_tensor(gate[:, 0:2], gcn[:, D:W], hb[:, bass.ds(3 * k, 2)], ALU.add)
                V.tensor_scalar(den[:, :], att[:, D:D + 1], 1e-5, None, ALU.add)
                dve.drain()
                V.tensor_tensor(gate[:, 0:2], gate[:, 0:2], gb_sb[:, :], ALU.add)
                V.tensor_tensor(work, gcn[:, 0:D], b_gcn, ALU.add)
                V.reciprocal(den[:, :], den[:, :])
                dve.drain()
                V.tensor_scalar(gate[:, 0:2], gate[:, 0:2], SIG_MIN, None, ALU.max).then_inc(gate_arg, 1)
                dve.wait_ge(gate_exp, k + 1)
                V.tensor_scalar(gate[:, 2:4], gate[:, 2:4], 1.0, None, ALU.add)
                dve.drain()
                V.reciprocal(gate[:, 2:4], gate[:, 2:4])
                dve.drain()
                V.tensor_tensor(den[:, :], den[:, :], gate[:, 2:3], ALU.mult)
                V.tensor_scalar(work, work, gate[:, 3:4], None, ALU.mult)
                dve.drain()
                V.scalar_tensor_tensor(out=work2, in0=att[:, 0:D], scalar=den[:, :], in1=work, op0=ALU.mult,
                                       op1=ALU.add)
                dve.drain()
                V.tensor_scalar(work2, work2, SIG_MIN, None, ALU.max).then_inc(comb_ready, 1)
                dve.wait_ge(comb_exp, k + 1)
                V.tensor_scalar(work2, work2, 1.0, None, ALU.add)
                dve.drain()
                V.reciprocal(work2, work2)
                dve.drain()
                dve.wait_ge(out_sent[par], 16 + 16 * (k // 2))
                V.tensor_tensor(out_st[par], work2, x1[:, bass.ds(k * D, D)], ALU.add).then_inc(out_ready, 1)

            def layer(k, par, begins, ends, ahead):
                if begins:
                    masked(k, par)
                dve.drain()
                if ahead:
                    scores(k + 1)
                if ends:
                    combine(k - 1, 1 - par)

            dve.wait_ge(sl_ready, 2)
            scores(0)
            steps(dve, layer)


INPUTS = ("x", "adj_t", "w1t", "w2", "w3", "u_all", "wh", "wg", "rows", "gate_bias")


def kernel(**inputs):
    import concourse.bacc as bacc
    from concourse.bass_utils import run_bass_kernel_spmd

    a = {k: np.asarray(v) for k, v in inputs.items()}
    f32 = np.float32

    x = np.zeros((NP, D), f32)
    x[:N] = a["x"]
    adj = np.zeros((NP, NP), f32)
    adj[:N, :N] = a["adj"]
    blocks = adj.reshape(NT, P, NT, P)

    def halves(b):
        return np.ascontiguousarray(b.reshape(NT, P, 2, HALF * P).transpose(0, 2, 1, 3)).reshape(
            2 * NT, P, HALF * P)

    def by_feature(w):
        return np.ascontiguousarray(w.reshape(2, P, -1).transpose(1, 0, 2)).reshape(P, -1)

    u = [a["L0_gnn_U1"][0], a["L0_gnn_U2"][0], a["L0_gnn_U1"][1], a["L0_gnn_U2"][1],
         a["L0_gnn_U3"][0], a["L0_gnn_U3"][1]]
    wa, wb = a["L1_gnn_Wa"][0], a["L1_gnn_Wb"][0]
    rows = np.concatenate([a["L0_gnn_gamma"], a["L0_gnn_beta"], a["L1_gnn_a_sa"][0], a["L1_gnn_b_gcnb"]])
    gate_bias = np.concatenate([a["L1_gnn_ba"], a["L1_gnn_bb"]])
    arrays = {
        "x": np.ascontiguousarray(x.reshape(NT, P, D).transpose(1, 0, 2)).reshape(P, NT * D),
        "adj_t": halves(blocks.transpose(0, 3, 2, 1)),
        "w1t": np.ascontiguousarray(a["L0_gnn_W1"].T),
        "w2": a["L0_gnn_W2"],
        "w3": a["L0_gnn_W3"],
        "u_all": np.concatenate([by_feature(w) for w in u], axis=1),
        "wh": by_feature(np.concatenate([a["L1_gnn_W_sa"], wa[D:, None], wb[D:, None],
                                             np.zeros((D, WH - D - 2), f32)], axis=1)),
        "wg": by_feature(np.concatenate([a["L1_gnn_W_gcnb"], wa[:D, None], wb[:D, None]], axis=1)),
        "rows": np.ascontiguousarray(np.broadcast_to(rows, (P, rows.size))),
        "gate_bias": np.ascontiguousarray(np.broadcast_to(gate_bias, (P, 2))),
    }
    nc = bacc.Bacc("TRN2", target_bir_lowering=False, num_devices=1)
    args, fed = [], {}
    for name in INPUTS:
        fed[f"in_{name}"] = np.ascontiguousarray(arrays[name])
        args.append(nc.dram_tensor(f"in_{name}", arrays[name].shape, F32, kind="ExternalInput").ap())
    out = nc.dram_tensor("out", (N, D), F32, kind="ExternalOutput").ap()
    build(nc, *args, out)
    r = run_bass_kernel_spmd(nc, [fed], core_ids=[0])
    return r.results[0]["out"]
```
